# Optimizing a Trainium2 kernel written in Bass

```python
import numpy as np
import jax
import jax.numpy as jnp

def _softmax(x, axis=-1):
    return jax.nn.softmax(x, axis=axis)

def _gelu(x):
    return jax.nn.gelu(x, approximate=True)

def _silu(x):
    return jax.nn.silu(x)

def _sigmoid(x):
    return jax.nn.sigmoid(x)

def _layernorm(x, axis=-1, eps=1e-05):
    m = jnp.mean(x, axis=axis, keepdims=True)
    v = jnp.var(x, axis=axis, keepdims=True)
    return (x - m) / jnp.sqrt(v + eps)

def _scatter_add(tgt, idx, src, axis=0):
    return tgt.at[idx].add(src)

def _segment_sum(src, seg, n):
    return jax.ops.segment_sum(src, seg, n)
kernel_name = 'mk_gnn_ffn_d1_gnn_r8_8cf8da'

def setup_inputs(seed: int=0):
    np.random.seed(seed)
    _w = jnp.asarray

    def _rec_inputs():
        import jax
        import jax.numpy as jnp
        _gk = jax.random.key(seed)
        x = -0.0002117 + 1 * jax.random.normal(jax.random.fold_in(_gk, 1), (12500, 256), jnp.float32)
        src = jax.random.randint(jax.random.fold_in(_gk, 2), (200000,), 0, 12500, jnp.int32)
        dst = jnp.minimum((12500 * jax.random.uniform(jax.random.fold_in(_gk, 3), (200000,)) ** 2.0).astype(jnp.int32), 99999)
        _o = jnp.argsort(dst, stable=True)
        src = src[_o]
        dst = dst[_o]
        return (x, src, dst)
    x, src, dst = _rec_inputs()

    def _L0_gnn_setup():
        import jax, jax.numpy as jnp
        import numpy as np
        N_NODES = 12500
        N_EDGES = 200000
        D = 256

        def _sage_layer(x, src, dst, inv_deg, W_self, W_neigh, b):
            agg = jax.ops.segment_sum(x[src], dst, num_segments=N_NODES)
            mean = agg * inv_deg[:, None]
            return x @ W_self + mean @ W_neigh + b
        key = jax.random.key(seed)
        ks = jax.random.split(key, 16)
        inp = {'features': jax.random.normal(ks[0], (N_NODES, D), dtype=jnp.float32), 'src': jax.random.randint(ks[1], (N_EDGES,), 0, N_NODES, dtype=jnp.int32), 'dst': jax.random.randint(ks[2], (N_EDGES,), 0, N_NODES, dtype=jnp.int32)}
        scale = 1.0 / np.sqrt(D)
        for i in range(3):
            inp[f'W{i}_self'] = jax.random.normal(ks[3 + 4 * i], (D, D), dtype=jnp.float32) * scale
            inp[f'W{i}_neigh'] = jax.random.normal(ks[4 + 4 * i], (D, D), dtype=jnp.float32) * scale
            inp[f'b{i}'] = jnp.zeros((D,), dtype=jnp.float32)
        return inp
    _L0_gnn_all = _L0_gnn_setup()
    _L0_gnn_in = {k: v for k, v in _L0_gnn_all.items() if k in ('W0_self', 'W0_neigh', 'b0', 'W1_self', 'W1_neigh', 'b1', 'W2_self', 'W2_neigh', 'b2')}
    del _L0_gnn_all

    def _L0_ffn_setup():
        import jax, jax.numpy as jnp
        import numpy as np
        B, S, D = (8, 512, 256)
        H = 4 * D
        CAPACITY = 0.5
        key = jax.random.key(seed)
        ks = jax.random.split(key, 6)
        x = jax.random.normal(ks[0], (B, S, D), dtype=jnp.float32)
        attention_mask = jnp.zeros((B, 1, 1, S), dtype=jnp.float32)
        wr = jax.random.normal(ks[1], (D, 1), dtype=jnp.float32) * 0.02
        br = jnp.zeros((1,), dtype=jnp.float32)
        w1 = jax.random.normal(ks[2], (D, H), dtype=jnp.float32) * 0.02
        b1 = jnp.zeros((H,), dtype=jnp.float32)
        w2 = jax.random.normal(ks[3], (H, D), dtype=jnp.float32) * 0.02
        b2 = jnp.zeros((D,), dtype=jnp.float32)
        return {'x': x, 'attention_mask': attention_mask, 'wr': wr, 'br': br, 'w1': w1, 'b1': b1, 'w2': w2, 'b2': b2}
    _L0_ffn_all = _L0_ffn_setup()
    _L0_ffn_in = {k: v for k, v in _L0_ffn_all.items() if k in ('attention_mask', 'wr', 'br', 'w1', 'b1', 'w2', 'b2')}
    del _L0_ffn_all
    return {'x': x, 'src': src, 'dst': dst, 'L0_gnn_W0_self': _L0_gnn_in['W0_self'], 'L0_gnn_W0_neigh': _L0_gnn_in['W0_neigh'], 'L0_gnn_b0': _L0_gnn_in['b0'], 'L0_gnn_W1_self': _L0_gnn_in['W1_self'], 'L0_gnn_W1_neigh': _L0_gnn_in['W1_neigh'], 'L0_gnn_b1': _L0_gnn_in['b1'], 'L0_gnn_W2_self': _L0_gnn_in['W2_self'], 'L0_gnn_W2_neigh': _L0_gnn_in['W2_neigh'], 'L0_gnn_b2': _L0_gnn_in['b2'], 'L0_ffn_attention_mask': _L0_ffn_in['attention_mask'], 'L0_ffn_wr': _L0_ffn_in['wr'], 'L0_ffn_br': _L0_ffn_in['br'], 'L0_ffn_w1': _L0_ffn_in['w1'], 'L0_ffn_b1': _L0_ffn_in['b1'], 'L0_ffn_w2': _L0_ffn_in['w2'], 'L0_ffn_b2': _L0_ffn_in['b2']}

def reference(x, src, dst, L0_gnn_W0_self, L0_gnn_W0_neigh, L0_gnn_b0, L0_gnn_W1_self, L0_gnn_W1_neigh, L0_gnn_b1, L0_gnn_W2_self, L0_gnn_W2_neigh, L0_gnn_b2, L0_ffn_attention_mask, L0_ffn_wr, L0_ffn_br, L0_ffn_w1, L0_ffn_b1, L0_ffn_w2, L0_ffn_b2):
    import jax
    import jax.numpy as jnp

    def _L0_gnn_ref(features, src, dst, W0_self, W0_neigh, b0, W1_self, W1_neigh, b1, W2_self, W2_neigh, b2):
        import jax, jax.numpy as jnp
        import numpy as np
        N_NODES = 12500
        N_EDGES = 200000
        D = 256

        def _sage_layer(x, src, dst, inv_deg, W_self, W_neigh, b):
            agg = jax.ops.segment_sum(x[src], dst, num_segments=N_NODES)
            mean = agg * inv_deg[:, None]
            return x @ W_self + mean @ W_neigh + b
        deg = jax.ops.segment_sum(jnp.ones_like(src, dtype=features.dtype), dst, num_segments=N_NODES)
        inv_deg = 1.0 / jnp.maximum(deg, 1.0)
        h = _sage_layer(features, src, dst, inv_deg, W0_self, W0_neigh, b0)
        h = jax.nn.relu(h)
        h = _sage_layer(h, src, dst, inv_deg, W1_self, W1_neigh, b1)
        h = jax.nn.relu(h)
        h = _sage_layer(h, src, dst, inv_deg, W2_self, W2_neigh, b2)
        return h

    def _L0_ffn_ref(x, attention_mask, wr, br, w1, b1, w2, b2):
        import jax, jax.numpy as jnp
        import numpy as np
        B, S, D = (8, 512, 256)
        H = 4 * D
        CAPACITY = 0.5
        b, s, d = x.shape
        weights = (jnp.einsum('bsd,do->bso', x, wr) + br)[..., 0]
        k = max(1, int(CAPACITY * s))
        kk = k - 1 if k > 1 else 1
        _, idx = jax.lax.top_k(weights, k)
        sel_idx = idx[:, :kk]
        sel = jnp.take_along_axis(x, sel_idx[:, :, None], axis=1)
        h = jax.nn.gelu(jnp.einsum('bkd,dh->bkh', sel, w1) + b1)
        y = jnp.einsum('bkh,hd->bkd', h, w2) + b2
        w_sel = jnp.take_along_axis(weights, sel_idx, axis=1)
        y = y * w_sel[..., None]
        batch_idx = jnp.arange(b)[:, None]
        processed = jnp.zeros_like(x).at[batch_idx, sel_idx].set(y)
        return processed + x
    x = x + _L0_gnn_ref(_layernorm(x, axis=-1), src, dst, L0_gnn_W0_self, L0_gnn_W0_neigh, L0_gnn_b0, L0_gnn_W1_self, L0_gnn_W1_neigh, L0_gnn_b1, L0_gnn_W2_self, L0_gnn_W2_neigh, L0_gnn_b2)
    x = x + _L0_ffn_ref(_layernorm(x, axis=-1)[None], L0_ffn_attention_mask, L0_ffn_wr, L0_ffn_br, L0_ffn_w1, L0_ffn_b1, L0_ffn_w2, L0_ffn_b2)[0]
    return x

_drawn_inputs = setup_inputs


def setup_inputs(seed=0):
    import zlib

    import numpy as np

    out = dict(_drawn_inputs(seed))
    spreads = {'L0_gnn_b0': (0.0, 0.1),
     'L0_gnn_b1': (0.0, 0.1),
     'L0_gnn_b2': (0.0, 0.1),
     'L0_ffn_b1': (0.0, 0.8),
     'L0_ffn_b2': (0.0, 0.8)}
    factors = {'L0_ffn_wr': 3.464, 'L0_ffn_w1': 7.937, 'L0_ffn_w2': 7.428}
    for name, (base, spread) in spreads.items():
        noise = np.random.default_rng([zlib.crc32(name.encode()), seed]).standard_normal(out[name].shape)
        drawn = base * np.exp(spread * noise) if base else spread * noise
        out[name] = jnp.asarray(drawn.astype(out[name].dtype))
    for name, factor in factors.items():
        out[name] = (out[name] * factor).astype(out[name].dtype)
    return out
```

```python
from contextlib import ExitStack

import numpy as np

import concourse.bass as bass
from concourse import mybir

ALU = mybir.AluOpType
ACT = mybir.ActivationFunctionType
AX = mybir.AxisListType
F32 = mybir.dt.float32
BF16 = mybir.dt.bfloat16
I32 = mybir.dt.int32

P = 128
PARTS = 3
RING = 16
GROUP = 4
LN_EPS = 1e-5
LAYERS = 3
PEEL = 4
LAST_LOOPED = 96
BATCH = 4


def gnn_ffn_program(nc, x, src, dst, w_self, w_neigh, b_gnn, wr, br, w1, b1, w2, b2, out):
    N, D = x.shape
    E = src.shape[0]
    H = w1.shape[1]
    KD, KH = D // P, H // P
    NT = -(-N // P)
    TAIL_ROWS = N - (NT - 1) * P
    TILES = -(-E // P)
    TAIL_EDGES = E - (TILES - 1) * P
    STEPS = TILES + NT - 1
    CHUNKS = -(-STEPS // P)
    PADDED = CHUNKS * P
    BLOCKS = PADDED // RING
    SELECTED = max(1, N // 2) - 1
    W_BITS = 17
    assert KD == 2 and NT > LAST_LOOPED + 1 and BLOCKS % 2 == 0 and TAIL_EDGES < P

    def rows(n):
        return TAIL_ROWS if isinstance(n, int) and n == NT - 1 else P

    table = [nc.dram_tensor(f"table{l}", (N, PARTS * D), BF16).ap() for l in range(LAYERS)]
    edge_rows = nc.dram_tensor("edge_rows", (TILES, 2 * P), I32).ap()
    idx_dram = nc.dram_tensor("idx_dram", (P, PADDED + 2 * RING), I32).ap()
    yw_dram = nc.dram_tensor("yw_dram", (N, D), F32).ap()

    with ExitStack() as ctx:
        def sb(name, shape, dt=F32):
            return ctx.enter_context(nc.sbuf_tensor(name, shape, dt))

        def psum(name, shape):
            return ctx.enter_context(nc.psum_tensor(name, shape, F32))

        def sem(name):
            return ctx.enter_context(nc.semaphore(name))

        resid = sb("resid", [P, NT, D])
        gath = sb("gath", [P, RING, PARTS * D], BF16)
        onehot = sb("onehot", [P, RING, P], BF16)
        dst_local = sb("dst_local", [P, PADDED])
        idx_ring = sb("idx_ring", [P, 2, RING], I32)
        win_end = sb("win_end", [1, NT + 1], I32)
        w_gnn = sb("w_gnn", [P, KD, 2, 2 * D])
        w_gnn2 = sb("w_gnn2", [P, KD, 2 * D])
        w1_sb = w_gnn[:].rearrange("p k l n -> p k (l n)")
        w2_sb = sb("w2_sb", [P, KH, D])
        bias = sb("bias", [P, LAYERS, D])
        b2_sb = sb("b2_sb", [P, D])
        b1_sb = sb("b1_sb", [P, KH])
        wr_sb = sb("wr_sb", [P, KD])
        br_sb = sb("br_sb", [P, 1])
        iota_row = sb("iota_row", [P, P])
        iota_col = sb("iota_col", [P, 1])
        step_no = sb("step_no", [P, CHUNKS])
        node_rev = sb("node_rev", [P, NT])
        ident = sb("ident", [P, P])
        zeros = sb("zeros", [P, D + 1], BF16)
        ones_bf = sb("ones_bf", [P, 1], BF16)
        ones = sb("ones", [P, P])
        xb = [sb(f"xb{p}", [P, D]) for p in range(2)]
        feat = [sb(f"feat{p}", [P, D]) for p in range(2)]
        x1 = [sb(f"x1_{p}", [P, D]) for p in range(2)]
        featT = [sb(f"featT{p}", [P, KD, P]) for p in range(2)]
        split = [sb(f"split{p}", [P, PARTS, D], BF16) for p in range(2)]
        rest = sb("rest", [P, D])
        hidT = [sb(f"hidT{p}", [P, KH, P]) for p in range(2)]
        yw = [sb(f"yw{p}", [P, D]) for p in range(2)]
        stats = [sb(f"stats{p}", [P, 6]) for p in range(2)]
        mv = [sb(f"mv{p}", [P, 2]) for p in range(2)]
        sd = [sb(f"sd{p}", [P, 1]) for p in range(2)]
        rstd = [sb(f"rstd{p}", [P, 1]) for p in range(2)]
        eps = sb("eps", [P, 1])
        deg = sb("deg", [P, 1])
        inv_deg = sb("inv_deg", [P, NT])
        weight = sb("weight", [P, NT])
        fin = [sb(f"fin{p}", [P, BATCH, D]) for p in range(2)]
        sel = sb("sel", [P, NT])

        agg = [psum(f"agg{p}", [P, 512]) for p in range(2)]
        tp = psum("tp", [P, KD, 256])
        hid = psum("hid", [P, 2, 512])
        yb = [psum(f"yb{p}", [P, 512]) for p in range(2)]

        at = [0]

        def scratch(cols, dt=F32):
            a = resid[:].rearrange("p n d -> p (n d)")[:, at[0]:at[0] + cols]
            at[0] += cols
            return a if dt == F32 else a.bitcast(dt)

        last_dst = scratch(TILES, I32)
        last_win = scratch(TILES, I32)
        last_winf = scratch(TILES)
        tile_win = scratch(TILES)
        tile_end = scratch(TILES)
        iota_tile = scratch(TILES)
        below = scratch(TILES)
        tile_of = scratch(CHUNKS)
        tile_of_i = scratch(CHUNKS, I32)
        win_base = scratch(CHUNKS)
        pad = scratch(P, I32)
        edge_i = scratch(CHUNKS * 2 * P, I32).rearrange("p (c e) -> p c e", e=2 * P)
        edge_f = scratch(CHUNKS * 2 * P).rearrange("p (c e) -> p c e", e=2 * P)
        idx_all = scratch(PADDED + 2 * RING, I32)
        win_cnt = scratch(1)
        win_endf = scratch(1)

        consts = sem("consts")
        w_loaded = sem("w_loaded")
        edges_stored = sem("edges_stored")
        last_loaded = sem("last_loaded")
        prep = sem("prep")
        bcast_ready = sem("bcast_ready")
        bcast_copied = sem("bcast_copied")
        ends_T = sem("ends_T")
        edges_gathered = sem("edges_gathered")
        edge_T = sem("edge_T")
        edge_T_copied = sem("edge_T_copied")
        steps_ready = sem("steps_ready")
        idx_stored = sem("idx_stored")
        idx_loaded = [sem(f"idx_loaded{h}") for h in range(2)]
        landed = [sem(f"landed{j}") for j in range(RING)]
        rows_ready = sem("rows_ready")
        slots_free = sem("slots_free")
        pool_turn = sem("pool_turn")
        dve_turn = sem("dve_turn")
        onehot_ready = sem("onehot_ready")
        agg_ready = sem("agg_ready")
        below_ready = sem("below_ready")
        tile_of_ready = sem("tile_of_ready")
        dst_ready = sem("dst_ready")
        ident_ready = sem("ident_ready")
        win0_ready = sem("win0_ready")
        x_loaded = [sem(f"x_loaded{p}") for p in range(2)]
        stats_ready = sem("stats_ready")
        mv_ready = sem("mv_ready")
        sd_ready = sem("sd_ready")
        rstd_ready = sem("rstd_ready")
        deg_ready = sem("deg_ready")
        inv_ready = sem("inv_ready")
        o_ready = sem("o_ready")
        x1_ready = sem("x1_ready")
        base_ready = sem("base_ready")
        feat_ready = sem("feat_ready")
        tp_ready = sem("tp_ready")
        featT_ready = sem("featT_ready")
        mm_ready = sem("mm_ready")
        hi_ready = sem("hi_ready")
        rest_ready = sem("rest_ready")
        self_ready = sem("self_ready")
        mid_ready = sem("mid_ready")
        lo_ready = sem("lo_ready")
        stored = [sem(f"stored{p}") for p in range(2)]
        w1_loaded = sem("w1_loaded")
        f1_ready = sem("f1_ready")
        gelu_ready = sem("gelu_ready")
        y_ready = sem("y_ready")
        weight_ready = sem("weight_ready")
        ysum_ready = sem("ysum_ready")
        yw_ready = sem("yw_ready")
        yw_stored = [sem(f"yw_stored{p}") for p in range(2)]
        sel_step = sem("sel_step")
        part_ready = sem("part_ready")
        total_ready = sem("total_ready")
        fin_loaded = [sem(f"fin_loaded{p}") for p in range(2)]
        fin_ready = sem("fin_ready")
        fin_stored = [sem(f"fin_stored{p}") for p in range(2)]

        N_CONSTS = 11
        N_WEIGHTS = 16 * (2 * LAYERS + LAYERS + 5)

        def upto(phase, n):
            return n + (phase * NT + 1)

        def over_windows(eng, depth, slot):
            for w in range(PEEL):
                slot(w, w // 2, w % 2)
            with eng.Fori(PEEL // 2, LAST_LOOPED // 2) as i:
                for p in range(2):
                    slot(i * 2 + p, i, p)
            for w in range(LAST_LOOPED, NT + depth):
                slot(w, w // 2, w % 2)

        def exists(n):
            return not isinstance(n, int) or 0 <= n < NT

        def earlier(half, p, delay):
            return half - (delay - p + 1) // 2

        def col(n):
            return bass.ds(n, 1) if not isinstance(n, int) else slice(n, n + 1)

        def window_rows(t, n):
            return t[n * P:n * P + rows(n), :] if isinstance(n, int) else t[bass.ds(n * P, P), :]

        TURNS = LAST_LOOPED // (2 * BATCH)

        def window_span(t, n):
            return t[bass.ds(n * P, BATCH * P), :].rearrange("(b p) d -> p b d", p=P)

        block = ctx.enter_context(nc.Block())

        @block.sync
        def _(sp):
            full = (TILES - 1) * P
            sp.dma_start(edge_rows[0:TILES - 1, 0:P],
                         src[0:full].rearrange("(t e) -> t e", e=P)).then_inc(edges_stored, 16)
            sp.dma_start(edge_rows[0:TILES - 1, P:2 * P],
                         dst[0:full].rearrange("(t e) -> t e", e=P)).then_inc(edges_stored, 16)
            sp.dma_start(edge_rows[TILES - 1:TILES, 0:TAIL_EDGES],
                         src[full:E].rearrange("(t e) -> t e", t=1)).then_inc(edges_stored, 16)
            sp.dma_start(edge_rows[TILES - 1:TILES, P:P + TAIL_EDGES],
                         dst[full:E].rearrange("(t e) -> t e", t=1)).then_inc(edges_stored, 16)
            with nc.allow_non_contiguous_dma("one destination per edge tile"):
                sp.dma_start(last_dst[0:1, 0:TILES - 1],
                             dst[0:full].rearrange("(t e) -> e t", e=P)[P - 1:P, :]).then_inc(last_loaded, 16)
            sp.wait_ge(consts, N_CONSTS)
            sp.dma_start(edge_rows[TILES - 1:TILES, TAIL_EDGES:P],
                         pad[0:1, 0:P - TAIL_EDGES]).then_inc(edges_stored, 16)
            sp.dma_start(edge_rows[TILES - 1:TILES, P + TAIL_EDGES:2 * P],
                         pad[0:1, TAIL_EDGES:P]).then_inc(edges_stored, 16)
            for l in range(LAYERS):
                w_l = w_gnn[:, :, l, :] if l < 2 else w_gnn2[:]
                for h, w in enumerate((w_neigh[l], w_self[l])):
                    sp.dma_start(w_l[:, :, h * D:(h + 1) * D],
                                 w.rearrange("(k p) n -> p k n", p=P)).then_inc(w_loaded, 16)
                sp.dma_start(bias[:, l, :], b_gnn[l].partition_broadcast(P)).then_inc(w_loaded, 16)
            sp.dma_start(w2_sb[:], w2.rearrange("(k p) n -> p k n", p=P)).then_inc(w_loaded, 16)
            sp.dma_start(b2_sb[:], b2.partition_broadcast(P)).then_inc(w_loaded, 16)
            sp.dma_start(br_sb[:], br.partition_broadcast(P)).then_inc(w_loaded, 16)
            with nc.allow_non_contiguous_dma("small vectors onto the partitions"):
                sp.dma_start(b1_sb[:], b1.rearrange("(k p) -> p k", p=P)).then_inc(w_loaded, 16)
                sp.dma_start(wr_sb[:], wr.rearrange("(k p) o -> p (k o)", p=P)).then_inc(w_loaded, 16)

            sp.wait_ge(steps_ready, 1)
            sp.dma_start(idx_dram[:, :], idx_all).then_inc(idx_stored, 16)
            sp.wait_ge(idx_stored, 16)
            for h in range(2):
                sp.dma_start(idx_ring[:, h, :], idx_dram[:, h * RING:(h + 1) * RING]).then_inc(idx_loaded[h], 16)

            def load_x(w, half, p):
                if not isinstance(w, int) or w >= 2:
                    sp.wait_ge(feat_ready, upto(0, w - 2))
                if exists(w):
                    sp.dma_start(xb[p][0:rows(w), :], window_rows(x, w)).then_inc(x_loaded[p], 16)
            over_windows(sp, 0, load_x)

            for layer in range(LAYERS):
                with sp.Fori(0, BLOCKS // 2) as it:
                    for h in range(2):
                        for j in range(RING):
                            sp.wait_ge(landed[j], it * 32 + 16 * (layer * BLOCKS + h + 1))
                            sp.sem_inc(rows_ready, 1)
                        sp.dma_start(idx_ring[:, h, :],
                                     idx_dram[:, bass.ds(it * (2 * RING) + (h + 2) * RING, RING)]
                                     ).then_inc(idx_loaded[h], 16)
            for h in range(2):
                sp.wait_ge(idx_loaded[h], 16 * (LAYERS * BLOCKS // 2 + 1))

            for p in range(2):
                sp.wait_ge(yw_stored[p], 16 * (NT // 2))

            def load_batch(it, p):
                sp.dma_start(fin[p][:],
                             window_span(yw_dram, it * (2 * BATCH) + p * BATCH)).then_inc(fin_loaded[p], 16)
            for p in range(2):
                load_batch(0, p)
            with sp.Fori(1, TURNS) as it:
                for p in range(2):
                    sp.wait_ge(fin_stored[p], it * 16)
                    load_batch(it, p)
            for p, n in enumerate(range(LAST_LOOPED, NT)):
                sp.wait_ge(fin_stored[p], 16 * TURNS)
                sp.dma_start(fin[p][0:rows(n), 0, :], window_rows(yw_dram, n)).then_inc(fin_loaded[p], 16)

        @block.gpsimd
        def _(pool):
            g = nc.gpsimd
            small = dict(allow_small_or_imprecise_dtypes=True)
            g.iota(iota_row[:], [[1, P]], base=0, channel_multiplier=0, **small).then_inc(consts, 1)
            g.iota(iota_col[:], [[1, 1]], base=0, channel_multiplier=1, **small).then_inc(consts, 1)
            g.iota(step_no[:], [[P, CHUNKS]], base=0, channel_multiplier=1, **small).then_inc(consts, 1)
            g.iota(node_rev[:], [[-P, NT]], base=N, channel_multiplier=-1, **small).then_inc(consts, 1)
            g.iota(iota_tile, [[1, TILES]], base=0, channel_multiplier=0, **small).then_inc(consts, 1)

            pool.wait_ge(edges_stored, 6 * 16)
            pool.wait_ge(prep, 9)
            for c in range(CHUNKS):
                g.indirect_dma_start(edge_i[:, c, :], None, edge_rows[:, :],
                                     bass.IndirectOffsetOnAxis(ap=tile_of_i[:, c:c + 1], axis=0)
                                     ).then_inc(edges_gathered, 16)

            for layer in range(LAYERS):
                for p in range(2):
                    pool.wait_ge(stored[p], 16 * (NT // 2) * (layer + 1))
                with pool.Fori(0, BLOCKS // 2) as it:
                    for h in range(2):
                        pool.wait_ge(idx_loaded[h], it * 16 + 16 * (layer * BLOCKS // 2 + 1))
                        for q in range(0, RING, GROUP):
                            pool.wait_ge(slots_free, it * (2 * RING) + (layer * PADDED + h * RING + q + GROUP))
                            pool.sem_inc(pool_turn, 1)
                            for j in range(q, q + GROUP):
                                g.indirect_dma_start(gath[:, j, :], None, table[layer][:, :],
                                                     bass.IndirectOffsetOnAxis(ap=idx_ring[:, h, j:j + 1], axis=0)
                                                     ).then_inc(landed[j], 16)

        @block.tensor
        def _(pe):
            mm = nc.tensor.matmul
            pe.sem_inc(slots_free, RING)
            pe.wait_ge(consts, N_CONSTS)
            pe.wait_ge(ident_ready, 1)

            pe.wait_ge(prep, 3)
            banks = [hid[:, 0, :], hid[:, 1, :], agg[0][:], agg[1][:]]
            for i in range(0, TILES, 512):
                n = min(512, TILES - i)
                mm(banks[i // 512][:, 0:n], ones[0:1, :], last_winf[0:1, i:i + n], start=True, stop=True
                   ).then_inc(bcast_ready, 1)
            pe.wait_ge(prep, 11)
            nc.tensor.transpose(tp[0:1, 0, 0:P], win_endf, ident[:]).then_inc(ends_T, 1)
            pe.wait_ge(dst_ready, CHUNKS)
            for c in range(CHUNKS):
                for h in range(2):
                    pe.wait_ge(edge_T_copied, c * 2 + (h + 1))
                    nc.tensor.transpose(yb[h][:, 0:P], edge_f[:, c, h * P:(h + 1) * P], ident[:]
                                        ).then_inc(edge_T, 1)
            pe.wait_ge(w_loaded, N_WEIGHTS)
            pe.wait_ge(edge_T_copied, CHUNKS * 2 + 2)

            def transposes(phase, n, p):
                pe.wait_ge(feat_ready, upto(phase, n))
                if phase or not isinstance(n, int) or n:
                    pe.wait_ge(featT_ready, upto(phase, n - 1))
                r = rows(n)
                for k in range(KD):
                    last = nc.tensor.transpose(tp[:, k, 0:r], feat[p][0:r, k * P:(k + 1) * P], ident[0:r, 0:r])
                last.then_inc(tp_ready, 1)

            def layer_product(phase, n, p):
                pe.wait_ge(featT_ready, upto(phase, n))
                if phase or not isinstance(n, int) or n >= 2:
                    pe.wait_ge(lo_ready, upto(phase, n - 2))
                r = rows(n)
                for k in range(KD):
                    w = w_gnn[:, k, phase, :] if phase < 2 else w_gnn2[:, k, :]
                    last = mm(yb[p][0:r, :], featT[p][:, k, 0:r], w, start=(k == 0), stop=(k == KD - 1))
                last.then_inc(mm_ready, 1)

            def aggregate(layer, n, p):
                lo = pe.value_load(win_end[0:1, col(n)], min_val=0, max_val=STEPS - 1)
                hi = pe.value_load(win_end[0:1, col(n + 1)], min_val=1, max_val=STEPS)
                g0 = layer * PADDED
                if layer == 2 and (not isinstance(n, int) or n >= 2):
                    pe.wait_ge(o_ready, n - 1)
                elif layer == 2:
                    pe.wait_ge(feat_ready, upto(2, NT - 2 + n))
                elif layer or not isinstance(n, int) or n >= 2:
                    pe.wait_ge(feat_ready, upto(layer + 1, n - 2))
                mm(agg[p][:, 0:D + 1], zeros[:, 0:P], zeros[:], start=True, stop=False, skip_group_check=True)
                with pe.Fori(lo, hi) as s:
                    slot = pe.snap(s % RING)
                    pe.wait_ge(onehot_ready, s + (layer * STEPS + 1))
                    pe.wait_ge(rows_ready, s + (g0 + 1))
                    oh = onehot[:, bass.ds(slot, 1), :]
                    if layer == 0:
                        mm(agg[p][:, D:D + 1], oh, ones_bf[:], start=False, stop=False, skip_group_check=True)
                    for part in range(PARTS):
                        last = mm(agg[p][:, 0:D], oh, gath[:, bass.ds(slot, 1), part * D:(part + 1) * D],
                                  start=False, stop=False, skip_group_check=True)
                    last.then_inc(slots_free, 1)
                if isinstance(n, int) and n == NT - 1:
                    pe.wait_ge(rows_ready, (layer + 1) * PADDED)
                    mm(agg[p][:, 0:1], zeros[:, 0:P], zeros[:, 0:1], start=False, stop=False,
                       skip_group_check=True).then_inc(slots_free, PADDED - STEPS)
                mm(agg[p][:, 0:1], zeros[:, 0:P], zeros[:, 0:1], start=False, stop=True, skip_group_check=True
                   ).then_inc(agg_ready, 1)

            def slot_table(w, half, p):
                if exists(w - 1):
                    transposes(0, w - 1, 1 - p)
                if exists(w - 2):
                    layer_product(0, w - 2, p)
            over_windows(pe, 2, slot_table)

            pe.wait_ge(steps_ready, 1)
            for layer in range(LAYERS - 1):
                def slot_layer(w, half, p, layer=layer):
                    if exists(w):
                        aggregate(layer, w, p)
                    if exists(w - 1):
                        transposes(layer + 1, w - 1, 1 - p)
                    if exists(w - 2):
                        layer_product(layer + 1, w - 2, p)
                over_windows(pe, 2, slot_layer)

            def ffn_up(n, p):
                pe.wait_ge(featT_ready, upto(3, n))
                if not isinstance(n, int) or n:
                    pe.wait_ge(gelu_ready, n)
                r = rows(n)
                for j in range(KH):
                    for k in range(KD):
                        last = mm(hid[:, j // 4, (j % 4) * P:(j % 4) * P + r], w1_sb[:, k, j * P:(j + 1) * P],
                                  featT[p][:, k, 0:r], start=(k == 0), stop=(k == KD - 1))
                last.then_inc(f1_ready, 1)

            def ffn_down(n, p):
                pe.wait_ge(gelu_ready, n + 1)
                if not isinstance(n, int) or n >= 2:
                    pe.wait_ge(yw_ready, n - 1)
                r = rows(n)
                for j in range(KH):
                    mm(yb[p][0:r, 0:D], hidT[p][:, j, 0:r], w2_sb[:, j, :], start=(j == 0), stop=(j == KH - 1))
                for k in range(KD):
                    last = mm(yb[p][0:r, D:D + 1], featT[p][:, k, 0:r], wr_sb[:, k:k + 1],
                              start=(k == 0), stop=(k == KD - 1))
                last.then_inc(y_ready, 1)

            pe.wait_ge(w1_loaded, 16)
            pe.wait_ge(lo_ready, upto(2, NT - 1))

            def slot_ffn(w, half, p):
                if exists(w):
                    aggregate(2, w, p)
                if exists(w - 2):
                    transposes(3, w - 2, p)
                if exists(w - 3):
                    ffn_down(w - 3, 1 - p)
                if exists(w - 2):
                    ffn_up(w - 2, p)
            over_windows(pe, 4, slot_ffn)

            with pe.Fori(0, 3 * W_BITS + 2) as i:
                pe.wait_ge(part_ready, i + 1)
                mm(tp[:, 0, 0:1], ones[:], deg[:], start=True, stop=True).then_inc(total_ready, 1)

        @block.vector
        def _(dve):
            v = nc.vector
            v.memset(zeros[:], 0.0).then_inc(consts, 1)
            v.memset(ones_bf[:], 1.0).then_inc(consts, 1)
            v.memset(ones[:], 1.0).then_inc(consts, 1)
            v.memset(eps[:], LN_EPS).then_inc(consts, 1)
            v.memset(pad[0:1, 0:TAIL_EDGES], 0).then_inc(consts, 1)
            v.memset(pad[0:1, TAIL_EDGES:P], N).then_inc(consts, 1)
            v.memset(last_dst[0:1, TILES - 1:TILES], N).then_inc(prep, 1)
            dve.wait_ge(consts, N_CONSTS)
            v.tensor_scalar(ident[:], iota_row[:], iota_col[:, 0:1], None, ALU.is_equal).then_inc(ident_ready, 1)
            dve.wait_ge(last_loaded, 16)
            dve.wait_ge(prep, 1)
            v.tensor_scalar(last_win[0:1, :], last_dst[0:1, :], 7, None, ALU.arith_shift_right).then_inc(prep, 1)
            dve.wait_ge(prep, 2)
            v.tensor_copy(last_winf[0:1, :], last_win[0:1, :]).then_inc(prep, 1)
            banks = [hid[:, 0, :], hid[:, 1, :], agg[0][:], agg[1][:]]
            for i in range(0, TILES, 512):
                n = min(512, TILES - i)
                dve.wait_ge(bcast_ready, i // 512 + 1)
                last = v.tensor_copy(tile_win[:, i:i + n], banks[i // 512][:, 0:n])
            last.then_inc(prep, 1)
            dve.wait_ge(prep, 4)
            v.tensor_tensor(tile_end, tile_win, iota_tile, ALU.add).then_inc(prep, 1)
            dve.wait_ge(prep, 5)
            with dve.Fori(0, CHUNKS) as c:
                v.tensor_scalar(below, tile_end, step_no[:, bass.ds(c, 1)], None, ALU.is_lt).then_inc(below_ready, 1)
                dve.wait_ge(below_ready, c + 1)
                v.tensor_reduce(tile_of[:, bass.ds(c, 1)], below, AX.X, ALU.add).then_inc(tile_of_ready, 1)
                dve.wait_ge(tile_of_ready, c + 1)
            v.tensor_scalar(tile_of, tile_of, float(TILES - 1), None, ALU.min).then_inc(prep, 1)
            dve.wait_ge(prep, 6)
            v.tensor_copy(tile_of_i, tile_of).then_inc(prep, 1)
            v.tensor_tensor(win_base, step_no[:], tile_of, ALU.subtract).then_inc(prep, 1)
            dve.wait_ge(prep, 8)
            v.tensor_scalar(win_base, win_base, float(P), None, ALU.mult).then_inc(prep, 1)
            v.tensor_scalar(below[:, 0:TILES - 1], tile_win[:, 0:TILES - 1], iota_col[:, 0:1], None,
                            ALU.is_le).then_inc(below_ready, 1)
            dve.wait_ge(below_ready, CHUNKS + 1)
            v.tensor_reduce(win_cnt, below[:, 0:TILES - 1], AX.X, ALU.add).then_inc(prep, 1)
            dve.wait_ge(prep, 10)
            v.tensor_scalar(win_endf, win_cnt, iota_col[:, 0:1], 1.0, ALU.add, ALU.add).then_inc(prep, 1)
            v.memset(win_end[0:1, 0:1], 0).then_inc(prep, 1)
            dve.wait_ge(ends_T, 1)
            v.tensor_copy(win_end[0:1, 1:NT + 1], tp[0:1, 0, 0:NT]).then_inc(prep, 1)
            dve.wait_ge(edges_gathered, 16 * CHUNKS)
            v.tensor_copy(edge_f, edge_i).then_inc(prep, 1)
            dve.wait_ge(prep, 14)
            with dve.Fori(0, CHUNKS) as c:
                d = edge_f[:, bass.ds(c, 1), P:2 * P]
                v.tensor_scalar(d, d, win_base[:, bass.ds(c, 1)], None, ALU.subtract).then_inc(dst_ready, 1)
            dve.sem_inc(edge_T_copied, 2)
            with dve.Fori(0, CHUNKS) as c:
                dve.wait_ge(edge_T, c * 2 + 1)
                v.tensor_copy(idx_all[:, bass.ds(c * P, P)], yb[0][:, 0:P]).then_inc(edge_T_copied, 1)
                dve.wait_ge(edge_T, c * 2 + 2)
                v.tensor_copy(dst_local[:, bass.ds(c * P, P)], yb[1][:, 0:P]).then_inc(edge_T_copied, 1)
            dve.wait_ge(edge_T_copied, 2 * CHUNKS + 2)
            v.tensor_copy(idx_all[:, PADDED:PADDED + 2 * RING], idx_all[:, 0:2 * RING]).then_inc(steps_ready, 1)
            v.memset(weight[:], 0.0).then_inc(prep, 1)
            dve.wait_ge(prep, 15)
            dve.wait_ge(w_loaded, N_WEIGHTS)
            dve.wait_ge(idx_stored, 16)

            def x_stats(phase, n, half, p, src_tile):
                v.bn_stats(stats[p][0:rows(n), :], src_tile).then_inc(stats_ready, 1)
                dve.wait_ge(stats_ready, n + (phase // 3 * NT + 1))
                dve.sem_inc(dve_turn, 1)
                v.bn_aggr(mv[p][0:rows(n), :], stats[p][0:rows(n), :]).then_inc(mv_ready, 1)

            def normalise(phase, n, p, src_tile):
                r = rows(n)
                at_n = n + (phase // 3 * NT + 1)
                dve.wait_ge(sd_ready, at_n)
                v.reciprocal(rstd[p][0:r, :], sd[p][0:r, :]).then_inc(rstd_ready, 1)
                dve.wait_ge(rstd_ready, at_n)
                if phase or not isinstance(n, int) or n >= 2:
                    dve.wait_ge(tp_ready, upto(phase, n - 2))
                v.tensor_scalar(feat[p][0:r, :], src_tile, mv[p][0:r, 0:1], rstd[p][0:r, 0:1],
                                ALU.subtract, ALU.mult).then_inc(feat_ready, 1)

            def split_product(phase, n, p):
                r = rows(n)
                dve.wait_ge(mm_ready, upto(phase, n))
                dve.wait_ge(hi_ready, upto(phase, n))
                if phase or not isinstance(n, int) or n:
                    dve.wait_ge(lo_ready, upto(phase, n - 1))
                v.tensor_tensor(rest[0:r, :], yb[p][0:r, 0:D], split[p][0:r, 0, :],
                                ALU.subtract).then_inc(rest_ready, 1)
                v.tensor_tensor(resid[0:r, col(n), :], yb[p][0:r, D:2 * D], bias[0:r, phase, :],
                                ALU.add).then_inc(self_ready, 1)
                dve.wait_ge(mid_ready, upto(phase, n))
                v.tensor_tensor(split[p][0:r, 2, :], rest[0:r, :], split[p][0:r, 1, :],
                                ALU.subtract).then_inc(lo_ready, 1)

            def slot_table(w, half, p):
                if exists(w):
                    dve.wait_ge(x_loaded[p], half * 16 + 16)
                    x_stats(0, w, half, p, xb[p][0:rows(w), :])
                if exists(w - 1):
                    normalise(0, w - 1, 1 - p, xb[1 - p][0:rows(w - 1), :])
                if exists(w - 2):
                    split_product(0, w - 2, p)
            over_windows(dve, 2, slot_table)

            def onehots(layer, n):
                lo = dve.value_load(win_end[0:1, col(n)], min_val=0, max_val=STEPS - 1)
                hi = dve.value_load(win_end[0:1, col(n + 1)], min_val=1, max_val=STEPS)
                with dve.Fori(lo, hi) as s:
                    dve.wait_ge(slots_free, s + (layer * PADDED + 1))
                    v.tensor_scalar(onehot[:, bass.ds(s % RING, 1), :], iota_row[:],
                                    dst_local[:, bass.ds(s, 1)], None, ALU.is_equal).then_inc(onehot_ready, 1)

            def aggregate_done(layer, n, p):
                r = rows(n)
                dve.wait_ge(agg_ready, n + (layer * NT + 1))
                if layer == 0:
                    v.tensor_scalar(deg[0:r, :], agg[p][0:r, D:D + 1], 1.0, None, ALU.max).then_inc(deg_ready, 1)
                    dve.wait_ge(deg_ready, n + 1)
                    v.reciprocal(inv_deg[0:r, col(n)], deg[0:r, :]).then_inc(inv_ready, 1)
                    dve.wait_ge(inv_ready, n + 1)
                o = feat[p] if layer < 2 else rest
                if layer < 2:
                    dve.wait_ge(tp_ready, upto(layer + 1, n - 2))
                v.scalar_tensor_tensor(out=o[0:r, :], in0=agg[p][0:r, 0:D], scalar=inv_deg[0:r, col(n)],
                                       in1=resid[0:r, col(n), :], op0=ALU.mult, op1=ALU.add
                                       ).then_inc(feat_ready if layer < 2 else o_ready, 1)

            for layer in range(LAYERS - 1):
                dve.wait_ge(self_ready, NT * (layer + 1))

                def slot_layer(w, half, p, layer=layer):
                    if exists(w - 1):
                        aggregate_done(layer, w - 1, 1 - p)
                    if exists(w):
                        onehots(layer, w)
                    if exists(w - 2):
                        split_product(layer + 1, w - 2, p)
                over_windows(dve, 2, slot_layer)

            dve.wait_ge(self_ready, NT * LAYERS)
            dve.wait_ge(lo_ready, NT * LAYERS)

            def ffn_result(n, p):
                r = rows(n)
                dve.wait_ge(y_ready, n + 1)
                v.tensor_scalar(weight[0:r, col(n)], yb[p][0:r, D:D + 1], br_sb[0:r, 0:1], None,
                                ALU.add).then_inc(weight_ready, 1)
                if not isinstance(n, int) or n:
                    dve.wait_ge(yw_ready, n)
                v.tensor_tensor(rest[0:r, :], yb[p][0:r, 0:D], b2_sb[0:r, :], ALU.add).then_inc(ysum_ready, 1)
                dve.wait_ge(weight_ready, n + 1)
                dve.wait_ge(ysum_ready, n + 1)

            def slot_ffn(w, half, p):
                if exists(w - 1):
                    n, q = w - 1, 1 - p
                    r = rows(n)
                    if not isinstance(n, int) or n >= 4:
                        dve.wait_ge(yw_ready, n - 3)
                    if not isinstance(n, int) or n >= 2:
                        dve.wait_ge(base_ready, n - 1)
                    aggregate_done(2, n, q)
                    dve.wait_ge(x_loaded[q], earlier(half, p, 1) * 16 + 16 * (NT // 2 + 1))
                    dve.wait_ge(o_ready, n + 1)
                    v.tensor_tensor(x1[q][0:r, :], rest[0:r, :], xb[q][0:r, :], ALU.add).then_inc(x1_ready, 1)
                    dve.wait_ge(x1_ready, n + 1)
                    x_stats(3, n, half, q, x1[q][0:r, :])
                if exists(w):
                    onehots(2, w)
                if exists(w - 1):
                    normalise(3, n, q, x1[q][0:r, :])
                    dve.wait_ge(feat_ready, upto(3, n))
                    v.tensor_tensor(resid[0:r, col(n), :], x1[q][0:r, :], feat[q][0:r, :],
                                    ALU.add).then_inc(base_ready, 1)
                if exists(w - 4):
                    ffn_result(w - 4, p)
                    m, rm = w - 4, rows(w - 4)
                    if not isinstance(m, int) or m >= 2:
                        dve.wait_ge(yw_stored[p], earlier(half, p, 4) * 16)
                    v.tensor_scalar(yw[p][0:rm, :], rest[0:rm, :], weight[0:rm, col(m)], None,
                                    ALU.mult).then_inc(yw_ready, 1)
            over_windows(dve, 4, slot_ffn)

            key, hi16, lo16 = (x1[0][:, 0:NT].bitcast(I32), x1[1][:, 0:NT].bitcast(I32), xb[0][:, 0:NT].bitcast(I32))
            low, cand = xb[1][:, 0:NT], feat[0][:, 0:NT]
            flag, exist = feat[1][:, 0:NT], rest[:, 0:NT]
            st = stats[0]
            thr, step, trial, wanted, gain = (st[:, i:i + 1] for i in range(5))
            count = [0]

            def link(ins, base=0):
                count[0] += 1
                ins.then_inc(sel_step, 1)
                dve.wait_ge(sel_step, base + count[0])

            dve.wait_ge(weight_ready, NT)
            dve.wait_ge(yw_ready, NT)
            dve.wait_ge(base_ready, NT)
            bits = weight[:].bitcast(I32)
            link(v.tensor_scalar(key, bits, 31, 0x7FFFFFFF, ALU.arith_shift_right, ALU.bitwise_and))
            link(v.tensor_tensor(key, key, bits, ALU.bitwise_xor))
            link(v.tensor_scalar(hi16, key, 16, None, ALU.arith_shift_right))
            link(v.tensor_scalar(lo16, key, 0xFFFF, None, ALU.bitwise_and))
            link(v.tensor_copy(cand, hi16))
            link(v.tensor_copy(low, lo16))
            link(v.tensor_scalar(exist, node_rev[:], 0.5, None, ALU.is_ge))
            link(v.tensor_scalar(cand, cand, float(2 ** 15 + 1), None, ALU.add))
            link(v.tensor_tensor(cand, cand, exist, ALU.mult))
            link(v.memset(sel[:], 0.0))
            link(v.memset(wanted, float(SELECTED)))
            totals = [0]

            def total_of(flags, base=0, done=0):
                v.tensor_reduce(deg[:], flags, AX.X, ALU.add).then_inc(part_ready, 1)
                dve.wait_ge(total_ready, base + done + 1)

            def search():
                link(v.memset(thr, 0.0))
                link(v.memset(step, float(2 ** (W_BITS - 1))))
                before, done = count[0], totals[0]
                PER_BIT = 5
                with dve.Fori(0, W_BITS) as i:
                    count[0] = 0
                    base = i * PER_BIT + before
                    link(v.tensor_tensor(trial, thr, step, ALU.add), base)
                    link(v.tensor_scalar(flag, cand, trial, None, ALU.is_ge), base)
                    total_of(flag, i, done)
                    link(v.tensor_scalar(gain, tp[:, 0, 0:1], wanted, step, ALU.is_ge, ALU.mult), base)
                    link(v.tensor_tensor(thr, thr, gain, ALU.add), base)
                    link(v.tensor_scalar(step, step, 0.5, None, ALU.mult), base)
                    assert count[0] == PER_BIT
                count[0] = before + PER_BIT * W_BITS
                totals[0] += W_BITS

            for rank, lower in enumerate((low, node_rev[:], None)):
                search()
                if lower is None:
                    link(v.tensor_scalar(flag, cand, thr, None, ALU.is_ge))
                    link(v.tensor_tensor(sel[:], sel[:], flag, ALU.add))
                    break
                link(v.tensor_scalar(flag, cand, thr, None, ALU.is_gt))
                link(v.tensor_tensor(sel[:], sel[:], flag, ALU.add))
                total_of(flag, 0, totals[0])
                totals[0] += 1
                link(v.tensor_tensor(wanted, wanted, tp[:, 0, 0:1], ALU.subtract))
                link(v.tensor_scalar(flag, cand, thr, None, ALU.is_equal))
                if rank == 0:
                    link(v.tensor_scalar(cand, lower, 1.0, None, ALU.add))
                    link(v.tensor_tensor(cand, cand, flag, ALU.mult))
                else:
                    link(v.tensor_tensor(cand, lower, flag, ALU.mult))
            assert totals[0] == 3 * W_BITS + 2

            def add_batch(it, p):
                for b in range(BATCH):
                    n = it * (2 * BATCH) + (p * BATCH + b)
                    last = v.scalar_tensor_tensor(out=fin[p][:, b, :], in0=fin[p][:, b, :], scalar=sel[:, col(n)],
                                                  in1=resid[:, col(n), :], op0=ALU.mult, op1=ALU.add)
                last.then_inc(fin_ready, 1)
            with dve.Fori(0, TURNS) as it:
                for p in range(2):
                    dve.wait_ge(fin_loaded[p], it * 16 + 16)
                    add_batch(it, p)
            for p, n in enumerate(range(LAST_LOOPED, NT)):
                r = rows(n)
                dve.wait_ge(fin_loaded[p], 16 * (TURNS + 1))
                v.scalar_tensor_tensor(out=fin[p][0:r, 0, :], in0=fin[p][0:r, 0, :], scalar=sel[0:r, n:n + 1],
                                       in1=resid[0:r, n, :], op0=ALU.mult, op1=ALU.add).then_inc(fin_ready, 1)

        @block.scalar
        def _(act):
            a = nc.scalar
            act.wait_ge(consts, N_CONSTS)

            def std_dev(phase, n, p):
                r = rows(n)
                act.wait_ge(mv_ready, n + (phase // 3 * NT + 1))
                a.activation(sd[p][0:r, :], mv[p][0:r, 1:2], ACT.Sqrt, bias=eps[0:r, 0:1]).then_inc(sd_ready, 1)

            def copy_transposed(phase, n, p):
                r = rows(n)
                act.wait_ge(tp_ready, upto(phase, n))
                if phase == 3 and (not isinstance(n, int) or n >= 2):
                    act.wait_ge(y_ready, n - 1)
                elif phase == 3:
                    act.wait_ge(mm_ready, NT * 3)
                elif phase or not isinstance(n, int) or n >= 2:
                    act.wait_ge(mm_ready, upto(phase, n - 2))
                func = ACT.Relu if phase in (1, 2) else ACT.Copy
                a.activation(featT[p][:, :, 0:r], tp[:, :, 0:r], func).then_inc(featT_ready, 1)

            def split_store(phase, n, half, p):
                r = rows(n)
                act.wait_ge(mm_ready, upto(phase, n))
                if phase or not isinstance(n, int) or n >= 2:
                    act.wait_ge(stored[p], half * 16 + 16 * phase * (NT // 2))
                a.copy(split[p][0:r, 0, :], yb[p][0:r, 0:D]).then_inc(hi_ready, 1)
                act.wait_ge(rest_ready, upto(phase, n))
                a.copy(split[p][0:r, 1, :], rest[0:r, :]).then_inc(mid_ready, 1)
                act.wait_ge(mid_ready, upto(phase, n))
                act.wait_ge(lo_ready, upto(phase, n))
                act.dma_start(window_rows(table[phase], n),
                              split[p][0:r, :, :].rearrange("p t d -> p (t d)")).then_inc(stored[p], 16)

            def slot_table(w, half, p):
                if exists(w):
                    std_dev(0, w, p)
                if exists(w - 1):
                    copy_transposed(0, w - 1, 1 - p)
                if exists(w - 2):
                    split_store(0, w - 2, earlier(half, p, 2), p)
            over_windows(act, 2, slot_table)

            for layer in range(LAYERS - 1):
                if layer == 1:
                    act.wait_ge(mm_ready, NT * 2)
                    act.dma_start(w1_sb, w1.rearrange("(k p) n -> p k n", p=P)).then_inc(w1_loaded, 16)

                def slot_layer(w, half, p, layer=layer):
                    if exists(w - 1):
                        copy_transposed(layer + 1, w - 1, 1 - p)
                    if exists(w - 2):
                        split_store(layer + 1, w - 2, earlier(half, p, 2), p)
                over_windows(act, 2, slot_layer)

            def gelu(n, p):
                r = rows(n)
                act.wait_ge(f1_ready, n + 1)
                if not isinstance(n, int) or n >= 2:
                    act.wait_ge(y_ready, n - 1)
                for j in range(KH):
                    last = a.activation(hidT[p][:, j, 0:r], hid[:, j // 4, (j % 4) * P:(j % 4) * P + r],
                                        ACT.Gelu_apprx_tanh, bias=b1_sb[:, j:j + 1])
                last.then_inc(gelu_ready, 1)

            act.wait_ge(feat_ready, upto(2, NT - 1))

            def slot_ffn(w, half, p):
                if exists(w):
                    if not isinstance(w, int) or w >= 2:
                        act.wait_ge(x1_ready, w - 1)
                    act.dma_start(xb[p][0:rows(w), :], window_rows(x, w)).then_inc(x_loaded[p], 16)
                if exists(w - 1):
                    std_dev(3, w - 1, 1 - p)
                if exists(w - 2):
                    copy_transposed(3, w - 2, p)
                    gelu(w - 2, p)
                if exists(w - 4):
                    act.wait_ge(yw_ready, w - 3)
                    act.dma_start(window_rows(yw_dram, w - 4), yw[p][0:rows(w - 4), :]).then_inc(yw_stored[p], 16)
            over_windows(act, 4, slot_ffn)

            with act.Fori(0, TURNS) as it:
                for p in range(2):
                    act.wait_ge(fin_ready, it * 2 + (p + 1))
                    act.dma_start(window_span(out, it * (2 * BATCH) + p * BATCH), fin[p][:]).then_inc(fin_stored[p], 16)
            for p, n in enumerate(range(LAST_LOOPED, NT)):
                act.wait_ge(fin_ready, 2 * TURNS + p + 1)
                act.dma_start(window_rows(out, n), fin[p][0:rows(n), 0, :]).then_inc(fin_stored[p], 16)
            for p in range(2):
                act.wait_ge(fin_stored[p], 16 * (TURNS + 1))


def kernel(x, src, dst, L0_gnn_W0_self, L0_gnn_W0_neigh, L0_gnn_b0, L0_gnn_W1_self, L0_gnn_W1_neigh, L0_gnn_b1,
           L0_gnn_W2_self, L0_gnn_W2_neigh, L0_gnn_b2, L0_ffn_attention_mask, L0_ffn_wr, L0_ffn_br, L0_ffn_w1,
           L0_ffn_b1, L0_ffn_w2, L0_ffn_b2):
    import concourse.bacc as bacc
    from concourse.bass_utils import run_bass_kernel_spmd

    nc = bacc.Bacc("TRN2", target_bir_lowering=False, num_devices=1)
    arrays = {}

    def give(name, a):
        a = np.ascontiguousarray(a)
        arrays[name] = a
        return nc.dram_tensor(name, a.shape, mybir.dt.from_np(a.dtype), kind="ExternalInput").ap()

    out = nc.dram_tensor("out", x.shape, F32, kind="ExternalOutput").ap()
    gnn_ffn_program(
        nc, give("x", x), give("src", src), give("dst", dst),
        [give(f"w_self{i}", w) for i, w in enumerate((L0_gnn_W0_self, L0_gnn_W1_self, L0_gnn_W2_self))],
        [give(f"w_neigh{i}", w) for i, w in enumerate((L0_gnn_W0_neigh, L0_gnn_W1_neigh, L0_gnn_W2_neigh))],
        [give(f"b_gnn{i}", b) for i, b in enumerate((L0_gnn_b0, L0_gnn_b1, L0_gnn_b2))],
        give("wr", L0_ffn_wr), give("br", L0_ffn_br), give("w1", L0_ffn_w1), give("b1", L0_ffn_b1),
        give("w2", L0_ffn_w2), give("b2", L0_ffn_b2), out)
    got = run_bass_kernel_spmd(nc, [arrays], core_ids=[0])
    return got.results[0]["out"]
```

```python
from contextlib import ExitStack

import numpy as np

import concourse.bass as bass
from concourse import mybir

ALU = mybir.AluOpType
ACT = mybir.ActivationFunctionType
AX = mybir.AxisListType
F32 = mybir.dt.float32
BF16 = mybir.dt.bfloat16
I32 = mybir.dt.int32

P = 128
PARTS = 3
GROUP = 4
RING = 16
RING_BLOCKS = RING // GROUP
LN_EPS = 1e-5
LAYERS = 3
PEEL = 4
LAST_LOOPED = 96
BATCH = 4


def gnn_ffn_program(nc, x, src, dst, w_self, w_neigh, b_gnn, wr, br, w1, b1, w2, b2, out):
    N, D = x.shape
    E = src.shape[0]
    H = w1.shape[1]
    KD, KH = D // P, H // P
    NT = -(-N // P)
    TAIL_ROWS = N - (NT - 1) * P
    TILES = -(-E // P)
    TAIL_EDGES = E - (TILES - 1) * P
    BLOCKS = -(-TILES // GROUP)
    TURN_TILES = 2 * RING
    PADDED = -(-TILES // TURN_TILES) * TURN_TILES
    PADDED_BLOCKS = PADDED // GROUP
    TURNS_PER_LAYER = PADDED // TURN_TILES
    PAIRS = BLOCKS + NT - 1
    CHUNKS = -(-PADDED // P)
    WHOLE = TILES // P
    SELECTED = max(1, N // 2) - 1
    W_BITS = 17
    assert KD == 2 and NT > LAST_LOOPED + 1 and TAIL_EDGES < P and PADDED_BLOCKS > BLOCKS

    def rows(n):
        return TAIL_ROWS if isinstance(n, int) and n == NT - 1 else P

    table = [nc.dram_tensor(f"table{l}", (N, PARTS * D), BF16).ap() for l in range(LAYERS)]
    idx_dram = nc.dram_tensor("idx_dram", (P, PADDED + 2 * RING), I32).ap()
    yw_dram = nc.dram_tensor("yw_dram", (N, D), F32).ap()

    with ExitStack() as ctx:
        def sb(name, shape, dt=F32):
            return ctx.enter_context(nc.sbuf_tensor(name, shape, dt))

        def psum(name, shape):
            return ctx.enter_context(nc.psum_tensor(name, shape, F32))

        def sem(name):
            return ctx.enter_context(nc.semaphore(name))

        resid = sb("resid", [P, NT, D])
        gath = sb("gath", [P, RING, PARTS * D + 2], BF16)
        onehot = [sb(f"onehot{p}", [P, RING, P], BF16) for p in range(2)]
        dst_f = sb("dst_f", [P, CHUNKS * P])
        idx_ring = sb("idx_ring", [P, 2, RING], I32)
        win_block = sb("win_block", [1, NT + 1], I32)
        w_gnn = sb("w_gnn", [P, KD, 2, 2 * D])
        w_gnn2 = sb("w_gnn2", [P, KD, 2 * D])
        w1_sb = w_gnn[:].rearrange("p k l n -> p k (l n)")
        w2_sb = sb("w2_sb", [P, KH, D])
        bias = sb("bias", [P, LAYERS, D])
        b2_sb = sb("b2_sb", [P, D])
        b1_sb = sb("b1_sb", [P, KH])
        wr_sb = sb("wr_sb", [P, KD])
        br_sb = sb("br_sb", [P, 1])
        iota_row = sb("iota_row", [P, P])
        iota_col = sb("iota_col", [P, 1])
        window_ids = [sb(f"window_ids{p}", [P, P]) for p in range(2)]
        node_rev = sb("node_rev", [P, NT])
        window_base = sb("window_base", [P, NT])
        ident = sb("ident", [P, P])
        zeros = sb("zeros", [P, 2 * D], BF16)
        ones = sb("ones", [P, P])
        xb = [sb(f"xb{p}", [P, D]) for p in range(2)]
        feat = [sb(f"feat{p}", [P, D]) for p in range(2)]
        x1 = [sb(f"x1_{p}", [P, D]) for p in range(2)]
        featT = [sb(f"featT{p}", [P, KD, P]) for p in range(2)]
        split = [sb(f"split{p}", [P, PARTS, D], BF16) for p in range(2)]
        rest = sb("rest", [P, D])
        hidT = [sb(f"hidT{p}", [P, KH, P]) for p in range(2)]
        yw = [sb(f"yw{p}", [P, D]) for p in range(2)]
        stats = [sb(f"stats{p}", [P, 6]) for p in range(2)]
        mv = [sb(f"mv{p}", [P, 2]) for p in range(2)]
        sd = [sb(f"sd{p}", [P, 1]) for p in range(2)]
        rstd = [sb(f"rstd{p}", [P, 1]) for p in range(2)]
        eps = sb("eps", [P, 1])
        deg = sb("deg", [P, 1])
        inv_deg = sb("inv_deg", [P, NT])
        weight = sb("weight", [P, NT])
        fin = [sb(f"fin{p}", [P, BATCH, D]) for p in range(2)]
        sel = sb("sel", [P, NT])

        agg = [psum(f"agg{p}", [P, 2, D]) for p in range(2)]
        agg_lo = [psum(f"agg_lo{p}", [P, 512]) for p in range(2)]
        tp = psum("tp", [P, KD, 256])
        hid = psum("hid", [P, 2, 512])
        y0 = psum("y0", [P, 512])
        yb = [y0[:], hid[:, 0, :]]

        at = [0]

        def scratch(cols, dt=F32):
            a = resid[:].rearrange("p n d -> p (n d)")[:, at[0]:at[0] + cols]
            at[0] += cols
            return a if dt == F32 else a.bitcast(dt)

        last_dst = scratch(BLOCKS, I32)
        last_win = scratch(BLOCKS, I32)
        last_winf = scratch(BLOCKS)
        before = scratch(BLOCKS)
        edge_i = scratch(2 * CHUNKS * P, I32).rearrange("p (s c e) -> p s c e", s=2, e=P)
        edge_f = scratch(2 * CHUNKS * P).rearrange("p (s c e) -> p s c e", s=2, e=P)
        idx_all = scratch(CHUNKS * P, I32)
        win_cnt = scratch(1)

        consts = sem("consts")
        w_loaded = sem("w_loaded")
        edges_loaded = sem("edges_loaded")
        last_loaded = sem("last_loaded")
        prep = sem("prep")
        bcast_ready = sem("bcast_ready")
        ends_T = sem("ends_T")
        edge_T = sem("edge_T")
        edge_T_copied = sem("edge_T_copied")
        steps_ready = sem("steps_ready")
        ids_ready = sem("ids_ready")
        lo_added = sem("lo_added")
        mid_added = sem("mid_added")
        idx_stored = sem("idx_stored")
        idx_loaded = [sem(f"idx_loaded{h}") for h in range(2)]
        landed = [sem(f"landed{j}") for j in range(RING)]
        rows_ready = sem("rows_ready")
        slots_free = sem("slots_free")
        pool_turn = sem("pool_turn")
        dve_turn = sem("dve_turn")
        onehot_ready = sem("onehot_ready")
        agg_ready = sem("agg_ready")
        ident_ready = sem("ident_ready")
        x_loaded = [sem(f"x_loaded{p}") for p in range(2)]
        stats_ready = sem("stats_ready")
        mv_ready = sem("mv_ready")
        sd_ready = sem("sd_ready")
        rstd_ready = sem("rstd_ready")
        deg_ready = sem("deg_ready")
        inv_ready = sem("inv_ready")
        o_ready = sem("o_ready")
        x1_ready = sem("x1_ready")
        base_ready = sem("base_ready")
        feat_ready = sem("feat_ready")
        tp_ready = sem("tp_ready")
        featT_ready = sem("featT_ready")
        mm_ready = sem("mm_ready")
        hi_ready = sem("hi_ready")
        rest_ready = sem("rest_ready")
        self_ready = sem("self_ready")
        mid_ready = sem("mid_ready")
        lo_ready = sem("lo_ready")
        stored = [sem(f"stored{p}") for p in range(2)]
        w1_loaded = sem("w1_loaded")
        f1_ready = sem("f1_ready")
        gelu_ready = sem("gelu_ready")
        y_ready = sem("y_ready")
        weight_ready = sem("weight_ready")
        ysum_ready = sem("ysum_ready")
        yw_ready = sem("yw_ready")
        yw_stored = [sem(f"yw_stored{p}") for p in range(2)]
        sel_step = sem("sel_step")
        part_ready = sem("part_ready")
        total_ready = sem("total_ready")
        fin_loaded = [sem(f"fin_loaded{p}") for p in range(2)]
        fin_ready = sem("fin_ready")
        fin_stored = [sem(f"fin_stored{p}") for p in range(2)]

        N_CONSTS = 10
        N_WEIGHTS = 16 * (2 * LAYERS + LAYERS + 5)

        def upto(phase, n):
            return n + (phase * NT + 1)

        def over_windows(eng, depth, slot):
            for w in range(PEEL):
                slot(w, w // 2, w % 2)
            with eng.Fori(PEEL // 2, LAST_LOOPED // 2) as i:
                for p in range(2):
                    slot(i * 2 + p, i, p)
            for w in range(LAST_LOOPED, NT + depth):
                slot(w, w // 2, w % 2)

        def exists(n):
            return not isinstance(n, int) or 0 <= n < NT

        def earlier(half, p, delay):
            return half - (delay - p + 1) // 2

        def col(n):
            return bass.ds(n, 1) if not isinstance(n, int) else slice(n, n + 1)

        def window_rows(t, n):
            return t[n * P:n * P + rows(n), :] if isinstance(n, int) else t[bass.ds(n * P, P), :]

        TURNS = LAST_LOOPED // (2 * BATCH)

        def window_span(t, n):
            return t[bass.ds(n * P, BATCH * P), :].rearrange("(b p) d -> p b d", p=P)

        block = ctx.enter_context(nc.Block())

        @block.sync
        def _(sp):
            whole, done = WHOLE * P * P, (TILES - 1) * P
            sp.wait_ge(consts, N_CONSTS)
            for h, e in enumerate((src, dst)):
                sp.dma_start(edge_i[:, h, 0:WHOLE, :],
                             e[0:whole].rearrange("(c p e) -> p c e", p=P, e=P)).then_inc(edges_loaded, 16)
                sp.dma_start(edge_i[0:TILES - 1 - WHOLE * P, h, WHOLE, :],
                             e[whole:done].rearrange("(t e) -> t e", e=P)).then_inc(edges_loaded, 16)
                row = TILES - 1 - WHOLE * P
                sp.dma_start(edge_i[row:row + 1, h, WHOLE, 0:TAIL_EDGES],
                             e[done:E].rearrange("(t e) -> t e", t=1)).then_inc(edges_loaded, 16)
            with nc.allow_non_contiguous_dma("one destination per block"):
                sp.dma_start(last_dst[0:1, 0:BLOCKS - 1],
                             dst[0:(BLOCKS - 1) * GROUP * P].rearrange("(b e) -> e b", e=GROUP * P)
                             [GROUP * P - 1:GROUP * P, :]).then_inc(last_loaded, 16)
            for l in range(LAYERS):
                w_l = w_gnn[:, :, l, :] if l < 2 else w_gnn2[:]
                for h, w in enumerate((w_neigh[l], w_self[l])):
                    sp.dma_start(w_l[:, :, h * D:(h + 1) * D],
                                 w.rearrange("(k p) n -> p k n", p=P)).then_inc(w_loaded, 16)
                sp.dma_start(bias[:, l, :], b_gnn[l].partition_broadcast(P)).then_inc(w_loaded, 16)
            sp.dma_start(w2_sb[:], w2.rearrange("(k p) n -> p k n", p=P)).then_inc(w_loaded, 16)
            sp.dma_start(b2_sb[:], b2.partition_broadcast(P)).then_inc(w_loaded, 16)
            sp.dma_start(br_sb[:], br.partition_broadcast(P)).then_inc(w_loaded, 16)
            with nc.allow_non_contiguous_dma("small vectors onto the partitions"):
                sp.dma_start(b1_sb[:], b1.rearrange("(k p) -> p k", p=P)).then_inc(w_loaded, 16)
                sp.dma_start(wr_sb[:], wr.rearrange("(k p) o -> p (k o)", p=P)).then_inc(w_loaded, 16)

            sp.wait_ge(steps_ready, 1)
            sp.dma_start(idx_dram[:, 0:PADDED], idx_all[:, 0:PADDED]).then_inc(idx_stored, 16)
            sp.dma_start(idx_dram[:, PADDED:PADDED + 2 * RING], idx_all[:, 0:2 * RING]).then_inc(idx_stored, 16)
            sp.wait_ge(idx_stored, 32)
            for h in range(2):
                sp.dma_start(idx_ring[:, h, :], idx_dram[:, h * RING:(h + 1) * RING]).then_inc(idx_loaded[h], 16)

            def load_x(w, half, p):
                if not isinstance(w, int) or w >= 2:
                    sp.wait_ge(feat_ready, upto(0, w - 2))
                if exists(w):
                    sp.dma_start(xb[p][0:rows(w), :], window_rows(x, w)).then_inc(x_loaded[p], 16)
            over_windows(sp, 0, load_x)

            for layer in range(LAYERS):
                with sp.Fori(0, TURNS_PER_LAYER) as it:
                    for h in range(2):
                        for j in range(RING):
                            sp.wait_ge(landed[j], it * 32 + 16 * (2 * layer * TURNS_PER_LAYER + h + 1))
                            if j % GROUP == GROUP - 1:
                                sp.sem_inc(rows_ready, 1)
                        sp.dma_start(idx_ring[:, h, :],
                                     idx_dram[:, bass.ds(it * TURN_TILES + (h + 2) * RING, RING)]
                                     ).then_inc(idx_loaded[h], 16)
            for h in range(2):
                sp.wait_ge(idx_loaded[h], 16 * (LAYERS * TURNS_PER_LAYER + 1))

            for p in range(2):
                sp.wait_ge(yw_stored[p], 16 * (NT // 2))

            def load_batch(it, p):
                sp.dma_start(fin[p][:],
                             window_span(yw_dram, it * (2 * BATCH) + p * BATCH)).then_inc(fin_loaded[p], 16)
            for p in range(2):
                load_batch(0, p)
            with sp.Fori(1, TURNS) as it:
                for p in range(2):
                    sp.wait_ge(fin_stored[p], it * 16)
                    load_batch(it, p)
            for p, n in enumerate(range(LAST_LOOPED, NT)):
                sp.wait_ge(fin_stored[p], 16 * TURNS)
                sp.dma_start(fin[p][0:rows(n), 0, :], window_rows(yw_dram, n)).then_inc(fin_loaded[p], 16)

        @block.gpsimd
        def _(pool):
            g = nc.gpsimd
            small = dict(allow_small_or_imprecise_dtypes=True)
            g.iota(iota_row[:], [[1, P]], base=0, channel_multiplier=0, **small).then_inc(consts, 1)
            g.iota(iota_col[:], [[1, 1]], base=0, channel_multiplier=1, **small).then_inc(consts, 1)
            g.iota(window_base[:], [[P, NT]], base=0, channel_multiplier=0, **small).then_inc(consts, 1)
            g.iota(node_rev[:], [[-P, NT]], base=N, channel_multiplier=-1, **small).then_inc(consts, 1)

            for layer in range(LAYERS):
                for p in range(2):
                    pool.wait_ge(stored[p], 16 * (NT // 2) * (layer + 1))
                with pool.Fori(0, TURNS_PER_LAYER) as it:
                    for h in range(2):
                        pool.wait_ge(idx_loaded[h], it * 16 + 16 * (layer * TURNS_PER_LAYER + 1))
                        for q in range(RING_BLOCKS):
                            pool.wait_ge(slots_free, it * (2 * RING_BLOCKS)
                                         + (layer * PADDED_BLOCKS + h * RING_BLOCKS + q + 1))
                            pool.sem_inc(pool_turn, 1)
                            for j in range(q * GROUP, (q + 1) * GROUP):
                                g.indirect_dma_start(gath[:, j, 0:PARTS * D], None, table[layer][:, :],
                                                     bass.IndirectOffsetOnAxis(ap=idx_ring[:, h, j:j + 1], axis=0)
                                                     ).then_inc(landed[j], 16)

        @block.tensor
        def _(pe):
            mm = nc.tensor.matmul
            pe.sem_inc(slots_free, RING_BLOCKS)
            pe.wait_ge(consts, N_CONSTS)
            pe.wait_ge(ident_ready, 1)

            pe.wait_ge(prep, 3)
            mm(y0[:, 0:BLOCKS - 1], ones[0:1, :], last_winf[0:1, 0:BLOCKS - 1], start=True, stop=True
               ).then_inc(bcast_ready, 1)
            pe.wait_ge(prep, 5)
            nc.tensor.transpose(tp[0:1, 0, 0:P], win_cnt, ident[:]).then_inc(ends_T, 1)
            pe.wait_ge(prep, 8)
            for c in range(CHUNKS):
                for h in range(2):
                    pe.wait_ge(edge_T_copied, c * 2 + (h + 1))
                    nc.tensor.transpose(yb[h][:, 0:P], edge_f[:, h, c, :], ident[:]).then_inc(edge_T, 1)
            pe.wait_ge(w_loaded, N_WEIGHTS)
            pe.wait_ge(edge_T_copied, CHUNKS * 2 + 2)

            def transposes(phase, n, p):
                pe.wait_ge(feat_ready, upto(phase, n))
                if phase or not isinstance(n, int) or n:
                    pe.wait_ge(featT_ready, upto(phase, n - 1))
                r = rows(n)
                for k in range(KD):
                    last = nc.tensor.transpose(tp[:, k, 0:r], feat[p][0:r, k * P:(k + 1) * P], ident[0:r, 0:r])
                last.then_inc(tp_ready, 1)

            def layer_product(phase, n, p):
                pe.wait_ge(featT_ready, upto(phase, n))
                if phase or not isinstance(n, int) or n >= 2:
                    pe.wait_ge(lo_ready, upto(phase, n - 2))
                r = rows(n)
                for k in range(KD):
                    w = w_gnn[:, k, phase, :] if phase < 2 else w_gnn2[:, k, :]
                    last = mm(yb[p][0:r, :], featT[p][:, k, 0:r], w, start=(k == 0), stop=(k == KD - 1))
                last.then_inc(mm_ready, 1)

            def aggregate(layer, n, p):
                first = pe.value_load(win_block[0:1, col(n)], min_val=0, max_val=BLOCKS - 1)
                shared = pe.value_load(win_block[0:1, col(n + 1)], min_val=0, max_val=BLOCKS - 1)
                if layer == 2 and (not isinstance(n, int) or n >= 2):
                    pe.wait_ge(o_ready, n - 1)
                elif layer == 2:
                    pe.wait_ge(feat_ready, upto(2, NT - 2 + n))
                elif layer or not isinstance(n, int) or n >= 2:
                    pe.wait_ge(feat_ready, upto(layer + 1, n - 2))
                lo_cols = D + 1 if layer == 0 else D
                hi_mid = agg[p][:].rearrange("p a d -> p (a d)")
                free = dict(stop=False, skip_group_check=True)
                mm(hi_mid, zeros[:, 0:P], zeros[:, 0:2 * D], start=True, **free)
                mm(agg_lo[p][:, 0:lo_cols], zeros[:, 0:P], zeros[:, 0:lo_cols], start=True, **free)

                def block_products(b):
                    base = pe.snap((b % RING_BLOCKS) * GROUP)
                    pe.wait_ge(onehot_ready, b + n + (layer * PAIRS + 1))
                    pe.wait_ge(rows_ready, b + (layer * PADDED_BLOCKS + 1))
                    for j in range(GROUP):
                        oh = onehot[p][:, bass.ds(base + j, 1), :]
                        tile_rows = gath[:, bass.ds(base + j, 1), :]
                        mm(hi_mid, oh, tile_rows[:, :, 0:2 * D], start=False, **free)
                        last = mm(agg_lo[p][:, 0:lo_cols], oh, tile_rows[:, :, 2 * D:2 * D + lo_cols],
                                  start=False, **free)
                    return last
                with pe.If(first < shared):
                    with pe.Fori(first, shared) as b:
                        block_products(b).then_inc(slots_free, 1)
                block_products(shared)
                if isinstance(n, int) and n == NT - 1:
                    pe.wait_ge(rows_ready, (layer + 1) * PADDED_BLOCKS)
                    mm(agg[p][:, 0, 0:1], zeros[:, 0:P], zeros[:, 0:1], start=False, **free
                       ).then_inc(slots_free, PADDED_BLOCKS - BLOCKS + 1)
                mm(agg[p][:, 0, 0:1], zeros[:, 0:P], zeros[:, 0:1], start=False, stop=True, skip_group_check=True
                   ).then_inc(agg_ready, 1)

            def slot_table(w, half, p):
                if exists(w - 1):
                    transposes(0, w - 1, 1 - p)
                if exists(w - 2):
                    layer_product(0, w - 2, p)
            over_windows(pe, 2, slot_table)

            pe.wait_ge(steps_ready, 1)
            for layer in range(LAYERS - 1):
                def slot_layer(w, half, p, layer=layer):
                    if exists(w - 3):
                        layer_product(layer + 1, w - 3, 1 - p)
                    if exists(w - 2):
                        transposes(layer + 1, w - 2, p)
                    if exists(w):
                        aggregate(layer, w, p)
                over_windows(pe, 3, slot_layer)

            def ffn_up(n, p):
                pe.wait_ge(featT_ready, upto(3, n))
                if not isinstance(n, int) or n:
                    pe.wait_ge(gelu_ready, n)
                r = rows(n)
                for j in range(KH):
                    for k in range(KD):
                        last = mm(hid[:, j // 4, (j % 4) * P:(j % 4) * P + r], w1_sb[:, k, j * P:(j + 1) * P],
                                  featT[p][:, k, 0:r], start=(k == 0), stop=(k == KD - 1))
                last.then_inc(f1_ready, 1)

            def ffn_down(n, p):
                pe.wait_ge(gelu_ready, n + 1)
                if not isinstance(n, int) or n:
                    pe.wait_ge(yw_ready, n)
                r = rows(n)
                for j in range(KH):
                    mm(y0[0:r, 0:D], hidT[p][:, j, 0:r], w2_sb[:, j, :], start=(j == 0), stop=(j == KH - 1))
                for k in range(KD):
                    last = mm(y0[0:r, D:D + 1], featT[p][:, k, 0:r], wr_sb[:, k:k + 1],
                              start=(k == 0), stop=(k == KD - 1))
                last.then_inc(y_ready, 1)

            pe.wait_ge(w1_loaded, 16)
            pe.wait_ge(lo_ready, upto(2, NT - 1))

            def slot_ffn(w, half, p):
                if exists(w - 2):
                    transposes(3, w - 2, p)
                if exists(w - 4):
                    ffn_down(w - 4, p)
                if exists(w - 3):
                    ffn_up(w - 3, 1 - p)
                if exists(w):
                    aggregate(2, w, p)
            over_windows(pe, 4, slot_ffn)

            with pe.Fori(0, 3 * W_BITS + 2) as i:
                pe.wait_ge(part_ready, i + 1)
                mm(tp[:, 0, 0:1], ones[:], deg[:], start=True, stop=True).then_inc(total_ready, 1)

        @block.vector
        def _(dve):
            v = nc.vector
            v.memset(zeros[:], 0.0).then_inc(consts, 1)
            v.memset(ones[:], 1.0).then_inc(consts, 1)
            v.memset(eps[:], LN_EPS).then_inc(consts, 1)
            v.memset(gath[:, :, PARTS * D:PARTS * D + 2], 1.0).then_inc(consts, 1)
            v.memset(edge_i[:, 0, WHOLE:CHUNKS, :], 0).then_inc(consts, 1)
            v.memset(edge_i[:, 1, WHOLE:CHUNKS, :], N).then_inc(consts, 1)
            dve.wait_ge(consts, N_CONSTS)
            v.tensor_scalar(ident[:], iota_row[:], iota_col[:, 0:1], None, ALU.is_equal).then_inc(ident_ready, 1)
            v.memset(win_block[0:1, 0:1], 0).then_inc(prep, 1)
            dve.wait_ge(last_loaded, 16)
            v.tensor_scalar(last_win[0:1, 0:BLOCKS - 1], last_dst[0:1, 0:BLOCKS - 1], P.bit_length() - 1, None,
                            ALU.arith_shift_right).then_inc(prep, 1)
            dve.wait_ge(prep, 2)
            v.tensor_copy(last_winf[0:1, 0:BLOCKS - 1], last_win[0:1, 0:BLOCKS - 1]).then_inc(prep, 1)
            dve.wait_ge(bcast_ready, 1)
            v.tensor_scalar(before[:, 0:BLOCKS - 1], y0[:, 0:BLOCKS - 1], iota_col[:, 0:1], None,
                            ALU.is_le).then_inc(prep, 1)
            dve.wait_ge(prep, 4)
            v.tensor_reduce(win_cnt, before[:, 0:BLOCKS - 1], AX.X, ALU.add).then_inc(prep, 1)
            dve.wait_ge(ends_T, 1)
            v.tensor_copy(win_block[0:1, 1:NT + 1], tp[0:1, 0, 0:NT]).then_inc(prep, 1)
            dve.wait_ge(edges_loaded, 6 * 16)
            for h in range(2):
                v.tensor_copy(edge_f[:, h, :, :], edge_i[:, h, :, :]).then_inc(prep, 1)
            dve.sem_inc(edge_T_copied, 2)
            with dve.Fori(0, CHUNKS) as c:
                at_c = dve.snap(c * P)
                dve.wait_ge(edge_T, c * 2 + 1)
                v.tensor_copy(idx_all[:, bass.ds(at_c, P)], yb[0][:, 0:P]).then_inc(edge_T_copied, 1)
                dve.wait_ge(edge_T, c * 2 + 2)
                v.tensor_copy(dst_f[:, bass.ds(at_c, P)], yb[1][:, 0:P]).then_inc(edge_T_copied, 1)
            dve.wait_ge(edge_T_copied, 2 * CHUNKS + 2)
            dve.sem_inc(steps_ready, 1)
            v.memset(weight[:], 0.0).then_inc(prep, 1)
            dve.wait_ge(prep, 9)
            dve.wait_ge(w_loaded, N_WEIGHTS)
            dve.wait_ge(idx_stored, 32)

            def x_stats(phase, n, half, p, src_tile):
                v.bn_stats(stats[p][0:rows(n), :], src_tile).then_inc(stats_ready, 1)
                dve.wait_ge(stats_ready, n + (phase // 3 * NT + 1))
                dve.sem_inc(dve_turn, 1)
                v.bn_aggr(mv[p][0:rows(n), :], stats[p][0:rows(n), :]).then_inc(mv_ready, 1)

            def normalise(phase, n, p, src_tile):
                r = rows(n)
                at_n = n + (phase // 3 * NT + 1)
                dve.wait_ge(sd_ready, at_n)
                v.reciprocal(rstd[p][0:r, :], sd[p][0:r, :]).then_inc(rstd_ready, 1)
                dve.wait_ge(rstd_ready, at_n)
                if phase or not isinstance(n, int) or n >= 2:
                    dve.wait_ge(tp_ready, upto(phase, n - 2))
                v.tensor_scalar(feat[p][0:r, :], src_tile, mv[p][0:r, 0:1], rstd[p][0:r, 0:1],
                                ALU.subtract, ALU.mult).then_inc(feat_ready, 1)

            def split_product(phase, n, p):
                r = rows(n)
                dve.wait_ge(mm_ready, upto(phase, n))
                dve.wait_ge(hi_ready, upto(phase, n))
                if phase or not isinstance(n, int) or n:
                    dve.wait_ge(lo_ready, upto(phase, n - 1))
                v.tensor_tensor(rest[0:r, :], yb[p][0:r, 0:D], split[p][0:r, 0, :],
                                ALU.subtract).then_inc(rest_ready, 1)
                v.tensor_tensor(resid[0:r, col(n), :], yb[p][0:r, D:2 * D], bias[0:r, phase, :],
                                ALU.add).then_inc(self_ready, 1)
                dve.wait_ge(mid_ready, upto(phase, n))
                v.tensor_tensor(split[p][0:r, 2, :], rest[0:r, :], split[p][0:r, 1, :],
                                ALU.subtract).then_inc(lo_ready, 1)

            def slot_table(w, half, p):
                if exists(w):
                    dve.wait_ge(x_loaded[p], half * 16 + 16)
                    x_stats(0, w, half, p, xb[p][0:rows(w), :])
                if exists(w - 1):
                    normalise(0, w - 1, 1 - p, xb[1 - p][0:rows(w - 1), :])
                if exists(w - 2):
                    split_product(0, w - 2, p)
            over_windows(dve, 2, slot_table)

            def onehots(layer, n, p):
                first = dve.value_load(win_block[0:1, col(n)], min_val=0, max_val=BLOCKS - 1)
                shared = dve.value_load(win_block[0:1, col(n + 1)], min_val=0, max_val=BLOCKS - 1)
                v.tensor_scalar(window_ids[p][:], iota_row[:], window_base[:, col(n)], None,
                                ALU.add).then_inc(ids_ready, 1)
                dve.wait_ge(ids_ready, n + (layer * NT + 1))
                dve.sem_inc(dve_turn, 1)

                def block_onehots(b):
                    slot, tiles = dve.snap((b % RING_BLOCKS) * GROUP), dve.snap(b * GROUP)
                    dve.wait_ge(slots_free, b + (layer * PADDED_BLOCKS + 1))
                    v.tensor_tensor(onehot[p][:, bass.ds(slot, GROUP), :],
                                    window_ids[p][:].unsqueeze(1).to_broadcast([P, GROUP, P]),
                                    dst_f[:, bass.ds(tiles, GROUP)].unsqueeze(2).to_broadcast([P, GROUP, P]),
                                    ALU.is_equal).then_inc(onehot_ready, 1)
                with dve.Fori(first, shared + 1) as b:
                    block_onehots(b)

            def aggregate_done(layer, n, p):
                r = rows(n)
                dve.wait_ge(agg_ready, n + (layer * NT + 1))
                if layer == 0:
                    v.tensor_scalar(deg[0:r, :], agg_lo[p][0:r, D:D + 1], 1.0, None, ALU.max).then_inc(deg_ready, 1)
                    dve.wait_ge(deg_ready, n + 1)
                    v.reciprocal(inv_deg[0:r, col(n)], deg[0:r, :]).then_inc(inv_ready, 1)
                    dve.wait_ge(inv_ready, n + 1)
                total, inv = resid[0:r, col(n), :], inv_deg[0:r, col(n)]
                for sums, added in ((agg_lo[p][0:r, 0:D], lo_added), (agg[p][0:r, 1, :], mid_added)):
                    v.scalar_tensor_tensor(out=total, in0=sums, scalar=inv, in1=total, op0=ALU.mult,
                                           op1=ALU.add).then_inc(added, 1)
                    dve.wait_ge(added, n + (layer * NT + 1))
                o = feat[p] if layer < 2 else rest
                if layer < 2:
                    dve.wait_ge(tp_ready, upto(layer + 1, n - 2))
                v.scalar_tensor_tensor(out=o[0:r, :], in0=agg[p][0:r, 0, :], scalar=inv, in1=total,
                                       op0=ALU.mult, op1=ALU.add
                                       ).then_inc(feat_ready if layer < 2 else o_ready, 1)

            for layer in range(LAYERS - 1):
                dve.wait_ge(self_ready, NT * (layer + 1))

                def slot_layer(w, half, p, layer=layer):
                    if exists(w):
                        onehots(layer, w, p)
                    if exists(w - 1):
                        aggregate_done(layer, w - 1, 1 - p)
                    if exists(w - 3):
                        split_product(layer + 1, w - 3, 1 - p)
                over_windows(dve, 3, slot_layer)

            dve.wait_ge(self_ready, NT * LAYERS)
            dve.wait_ge(lo_ready, NT * LAYERS)

            def ffn_result(n, half, p):
                r = rows(n)
                dve.wait_ge(y_ready, n + 1)
                v.tensor_scalar(weight[0:r, col(n)], y0[0:r, D:D + 1], br_sb[0:r, 0:1], None,
                                ALU.add).then_inc(weight_ready, 1)
                if not isinstance(n, int) or n >= 2:
                    dve.wait_ge(yw_stored[p], half * 16)
                v.tensor_tensor(yw[p][0:r, :], y0[0:r, 0:D], b2_sb[0:r, :], ALU.add).then_inc(ysum_ready, 1)
                dve.wait_ge(weight_ready, n + 1)
                dve.wait_ge(ysum_ready, n + 1)
                v.tensor_scalar(yw[p][0:r, :], yw[p][0:r, :], weight[0:r, col(n)], None,
                                ALU.mult).then_inc(yw_ready, 1)

            def slot_ffn(w, half, p):
                if exists(w):
                    onehots(2, w, p)
                if exists(w - 1):
                    n, q = w - 1, 1 - p
                    r = rows(n)
                    if not isinstance(n, int) or n >= 2:
                        dve.wait_ge(base_ready, n - 1)
                    aggregate_done(2, n, q)
                    dve.wait_ge(x_loaded[q], earlier(half, p, 1) * 16 + 16 * (NT // 2 + 1))
                    dve.wait_ge(o_ready, n + 1)
                    v.tensor_tensor(x1[q][0:r, :], rest[0:r, :], xb[q][0:r, :], ALU.add).then_inc(x1_ready, 1)
                    dve.wait_ge(x1_ready, n + 1)
                    x_stats(3, n, half, q, x1[q][0:r, :])
                    normalise(3, n, q, x1[q][0:r, :])
                    dve.wait_ge(feat_ready, upto(3, n))
                    v.tensor_tensor(resid[0:r, col(n), :], x1[q][0:r, :], feat[q][0:r, :],
                                    ALU.add).then_inc(base_ready, 1)
                if exists(w - 4):
                    ffn_result(w - 4, earlier(half, p, 4), p)
            over_windows(dve, 4, slot_ffn)

            key, hi16, lo16 = (x1[0][:, 0:NT].bitcast(I32), x1[1][:, 0:NT].bitcast(I32), xb[0][:, 0:NT].bitcast(I32))
            low, cand = xb[1][:, 0:NT], feat[0][:, 0:NT]
            flag, exist = feat[1][:, 0:NT], rest[:, 0:NT]
            st = stats[0]
            thr, step, trial, wanted, gain = (st[:, i:i + 1] for i in range(5))
            count = [0]

            def link(ins, base=0):
                count[0] += 1
                ins.then_inc(sel_step, 1)
                dve.wait_ge(sel_step, base + count[0])

            dve.wait_ge(weight_ready, NT)
            dve.wait_ge(yw_ready, NT)
            dve.wait_ge(base_ready, NT)
            bits = weight[:].bitcast(I32)
            link(v.tensor_scalar(key, bits, 31, 0x7FFFFFFF, ALU.arith_shift_right, ALU.bitwise_and))
            link(v.tensor_tensor(key, key, bits, ALU.bitwise_xor))
            link(v.tensor_scalar(hi16, key, 16, None, ALU.arith_shift_right))
            link(v.tensor_scalar(lo16, key, 0xFFFF, None, ALU.bitwise_and))
            link(v.tensor_copy(cand, hi16))
            link(v.tensor_copy(low, lo16))
            link(v.tensor_scalar(exist, node_rev[:], 0.5, None, ALU.is_ge))
            link(v.tensor_scalar(cand, cand, float(2 ** 15 + 1), None, ALU.add))
            link(v.tensor_tensor(cand, cand, exist, ALU.mult))
            link(v.memset(sel[:], 0.0))
            link(v.memset(wanted, float(SELECTED)))
            totals = [0]

            def total_of(flags, base=0, done=0):
                v.tensor_reduce(deg[:], flags, AX.X, ALU.add).then_inc(part_ready, 1)
                dve.wait_ge(total_ready, base + done + 1)

            def search():
                link(v.memset(thr, 0.0))
                link(v.memset(step, float(2 ** (W_BITS - 1))))
                before, done = count[0], totals[0]
                PER_BIT = 5
                with dve.Fori(0, W_BITS) as i:
                    count[0] = 0
                    base = i * PER_BIT + before
                    link(v.tensor_tensor(trial, thr, step, ALU.add), base)
                    link(v.tensor_scalar(flag, cand, trial, None, ALU.is_ge), base)
                    total_of(flag, i, done)
                    link(v.tensor_scalar(gain, tp[:, 0, 0:1], wanted, step, ALU.is_ge, ALU.mult), base)
                    link(v.tensor_tensor(thr, thr, gain, ALU.add), base)
                    link(v.tensor_scalar(step, step, 0.5, None, ALU.mult), base)
                    assert count[0] == PER_BIT
                count[0] = before + PER_BIT * W_BITS
                totals[0] += W_BITS

            for rank, lower in enumerate((low, node_rev[:], None)):
                search()
                if lower is None:
                    link(v.tensor_scalar(flag, cand, thr, None, ALU.is_ge))
                    link(v.tensor_tensor(sel[:], sel[:], flag, ALU.add))
                    break
                link(v.tensor_scalar(flag, cand, thr, None, ALU.is_gt))
                link(v.tensor_tensor(sel[:], sel[:], flag, ALU.add))
                total_of(flag, 0, totals[0])
                totals[0] += 1
                link(v.tensor_tensor(wanted, wanted, tp[:, 0, 0:1], ALU.subtract))
                link(v.tensor_scalar(flag, cand, thr, None, ALU.is_equal))
                if rank == 0:
                    link(v.tensor_scalar(cand, lower, 1.0, None, ALU.add))
                    link(v.tensor_tensor(cand, cand, flag, ALU.mult))
                else:
                    link(v.tensor_tensor(cand, lower, flag, ALU.mult))
            assert totals[0] == 3 * W_BITS + 2

            def add_batch(it, p):
                for b in range(BATCH):
                    n = it * (2 * BATCH) + (p * BATCH + b)
                    last = v.scalar_tensor_tensor(out=fin[p][:, b, :], in0=fin[p][:, b, :], scalar=sel[:, col(n)],
                                                  in1=resid[:, col(n), :], op0=ALU.mult, op1=ALU.add)
                last.then_inc(fin_ready, 1)
            with dve.Fori(0, TURNS) as it:
                for p in range(2):
                    dve.wait_ge(fin_loaded[p], it * 16 + 16)
                    add_batch(it, p)
            for p, n in enumerate(range(LAST_LOOPED, NT)):
                r = rows(n)
                dve.wait_ge(fin_loaded[p], 16 * (TURNS + 1))
                v.scalar_tensor_tensor(out=fin[p][0:r, 0, :], in0=fin[p][0:r, 0, :], scalar=sel[0:r, n:n + 1],
                                       in1=resid[0:r, n, :], op0=ALU.mult, op1=ALU.add).then_inc(fin_ready, 1)

        @block.scalar
        def _(act):
            a = nc.scalar
            act.wait_ge(consts, N_CONSTS)

            def std_dev(phase, n, p):
                r = rows(n)
                act.wait_ge(mv_ready, n + (phase // 3 * NT + 1))
                a.activation(sd[p][0:r, :], mv[p][0:r, 1:2], ACT.Sqrt, bias=eps[0:r, 0:1]).then_inc(sd_ready, 1)

            def copy_transposed(phase, n, p):
                r = rows(n)
                act.wait_ge(tp_ready, upto(phase, n))
                if phase == 3 and (not isinstance(n, int) or n >= 2):
                    act.wait_ge(y_ready, n - 1)
                elif phase == 3:
                    act.wait_ge(mm_ready, NT * 3)
                elif phase or not isinstance(n, int) or n >= 2:
                    act.wait_ge(mm_ready, upto(phase, n - 2))
                func = ACT.Relu if phase in (1, 2) else ACT.Copy
                a.activation(featT[p][:, :, 0:r], tp[:, :, 0:r], func).then_inc(featT_ready, 1)

            def split_store(phase, n, half, p):
                r = rows(n)
                act.wait_ge(mm_ready, upto(phase, n))
                if phase or not isinstance(n, int) or n >= 2:
                    act.wait_ge(stored[p], half * 16 + 16 * phase * (NT // 2))
                a.copy(split[p][0:r, 0, :], yb[p][0:r, 0:D]).then_inc(hi_ready, 1)
                act.wait_ge(rest_ready, upto(phase, n))
                a.copy(split[p][0:r, 1, :], rest[0:r, :]).then_inc(mid_ready, 1)
                act.wait_ge(mid_ready, upto(phase, n))
                act.wait_ge(lo_ready, upto(phase, n))
                act.dma_start(window_rows(table[phase], n),
                              split[p][0:r, :, :].rearrange("p t d -> p (t d)")).then_inc(stored[p], 16)

            def slot_table(w, half, p):
                if exists(w):
                    std_dev(0, w, p)
                if exists(w - 1):
                    copy_transposed(0, w - 1, 1 - p)
                if exists(w - 2):
                    split_store(0, w - 2, earlier(half, p, 2), p)
            over_windows(act, 2, slot_table)

            for layer in range(LAYERS - 1):
                if layer == 1:
                    act.wait_ge(mm_ready, NT * 2)
                    act.dma_start(w1_sb, w1.rearrange("(k p) n -> p k n", p=P)).then_inc(w1_loaded, 16)

                def slot_layer(w, half, p, layer=layer):
                    if exists(w - 2):
                        copy_transposed(layer + 1, w - 2, p)
                    if exists(w - 3):
                        split_store(layer + 1, w - 3, earlier(half, p, 3), 1 - p)
                over_windows(act, 3, slot_layer)

            def gelu(n, p):
                r = rows(n)
                act.wait_ge(f1_ready, n + 1)
                if not isinstance(n, int) or n >= 2:
                    act.wait_ge(y_ready, n - 1)
                for j in range(KH):
                    last = a.activation(hidT[p][:, j, 0:r], hid[:, j // 4, (j % 4) * P:(j % 4) * P + r],
                                        ACT.Gelu_apprx_tanh, bias=b1_sb[:, j:j + 1])
                last.then_inc(gelu_ready, 1)

            act.wait_ge(feat_ready, upto(2, NT - 1))

            def slot_ffn(w, half, p):
                if exists(w):
                    if not isinstance(w, int) or w >= 2:
                        act.wait_ge(x1_ready, w - 1)
                    act.dma_start(xb[p][0:rows(w), :], window_rows(x, w)).then_inc(x_loaded[p], 16)
                if exists(w - 1):
                    std_dev(3, w - 1, 1 - p)
                if exists(w - 2):
                    copy_transposed(3, w - 2, p)
                if exists(w - 3):
                    gelu(w - 3, 1 - p)
                if exists(w - 4):
                    act.wait_ge(yw_ready, w - 3)
                    act.dma_start(window_rows(yw_dram, w - 4), yw[p][0:rows(w - 4), :]).then_inc(yw_stored[p], 16)
            over_windows(act, 4, slot_ffn)

            with act.Fori(0, TURNS) as it:
                for p in range(2):
                    act.wait_ge(fin_ready, it * 2 + (p + 1))
                    act.dma_start(window_span(out, it * (2 * BATCH) + p * BATCH), fin[p][:]).then_inc(fin_stored[p], 16)
            for p, n in enumerate(range(LAST_LOOPED, NT)):
                act.wait_ge(fin_ready, 2 * TURNS + p + 1)
                act.dma_start(window_rows(out, n), fin[p][0:rows(n), 0, :]).then_inc(fin_stored[p], 16)
            for p in range(2):
                act.wait_ge(fin_stored[p], 16 * (TURNS + 1))


def kernel(x, src, dst, L0_gnn_W0_self, L0_gnn_W0_neigh, L0_gnn_b0, L0_gnn_W1_self, L0_gnn_W1_neigh, L0_gnn_b1,
           L0_gnn_W2_self, L0_gnn_W2_neigh, L0_gnn_b2, L0_ffn_attention_mask, L0_ffn_wr, L0_ffn_br, L0_ffn_w1,
           L0_ffn_b1, L0_ffn_w2, L0_ffn_b2):
    import concourse.bacc as bacc
    from concourse.bass_utils import run_bass_kernel_spmd

    nc = bacc.Bacc("TRN2", target_bir_lowering=False, num_devices=1)
    arrays = {}

    def give(name, a):
        a = np.ascontiguousarray(a)
        arrays[name] = a
        return nc.dram_tensor(name, a.shape, mybir.dt.from_np(a.dtype), kind="ExternalInput").ap()

    out = nc.dram_tensor("out", x.shape, F32, kind="ExternalOutput").ap()
    gnn_ffn_program(
        nc, give("x", x), give("src", src), give("dst", dst),
        [give(f"w_self{i}", w) for i, w in enumerate((L0_gnn_W0_self, L0_gnn_W1_self, L0_gnn_W2_self))],
        [give(f"w_neigh{i}", w) for i, w in enumerate((L0_gnn_W0_neigh, L0_gnn_W1_neigh, L0_gnn_W2_neigh))],
        [give(f"b_gnn{i}", b) for i, b in enumerate((L0_gnn_b0, L0_gnn_b1, L0_gnn_b2))],
        give("wr", L0_ffn_wr), give("br", L0_ffn_br), give("w1", L0_ffn_w1), give("b1", L0_ffn_b1),
        give("w2", L0_ffn_w2), give("b2", L0_ffn_b2), out)
    got = run_bass_kernel_spmd(nc, [arrays], core_ids=[0])
    return got.results[0]["out"]
```

```python
from contextlib import ExitStack

import numpy as np

import concourse.bass as bass
from concourse import mybir

ALU = mybir.AluOpType
ACT = mybir.ActivationFunctionType
AX = mybir.AxisListType
F32 = mybir.dt.float32
BF16 = mybir.dt.bfloat16
I32 = mybir.dt.int32

P = 128
PARTS = 3
GROUP = 4
RING = 16
RING_BLOCKS = RING // GROUP
LN_EPS = 1e-5
LAYERS = 3
PEEL = 6
LAST_LOOPED = 96
BATCH = 4
FIN_BUFS = 12


def gnn_ffn_program(nc, x, src, dst, w_self, w_neigh, b_gnn, wr, br, w1, b1, w2, b2, out):
    N, D = x.shape
    E = src.shape[0]
    H = w1.shape[1]
    KD, KH = D // P, H // P
    NT = -(-N // P)
    TAIL_ROWS = N - (NT - 1) * P
    TILES = -(-E // P)
    TAIL_EDGES = E - (TILES - 1) * P
    BLOCKS = -(-TILES // GROUP)
    TURN_TILES = 2 * RING
    PADDED = -(-TILES // TURN_TILES) * TURN_TILES
    PADDED_BLOCKS = PADDED // GROUP
    TURNS_PER_LAYER = PADDED // TURN_TILES
    PAIRS = BLOCKS + NT - 1
    CHUNKS = -(-PADDED // P)
    WHOLE = TILES // P
    SELECTED = max(1, N // 2) - 1
    DIGIT = 3
    TRIALS = 2 ** DIGIT - 1
    ROUNDS = (6, 6, 5)
    BATCHES = NT // BATCH + 1
    BLOCK_BITS = BLOCKS.bit_length()
    assert 3 * BLOCK_BITS < 31 and NT % 2 == 0
    assert NT == LAST_LOOPED + 2 and BATCHES % 4 == 1 and RING == 4 * BATCH
    FFN_ROUNDS = 6
    assert ROUNDS[0] == FFN_ROUNDS
    assert N < 2 ** (DIGIT * ROUNDS[2]) and LAST_LOOPED % (BATCH * FIN_BUFS) == 0
    assert KD == 2 and NT > LAST_LOOPED + 1 and TAIL_EDGES < P and PADDED_BLOCKS > BLOCKS

    def rows(n):
        return TAIL_ROWS if isinstance(n, int) and n == NT - 1 else P

    table = [nc.dram_tensor(f"table{l}", (N, PARTS * D), BF16).ap() for l in range(LAYERS)]
    idx_dram = nc.dram_tensor("idx_dram", (P, PADDED + 2 * RING), I32).ap()
    yw_dram = nc.dram_tensor("yw_dram", (N, D), F32).ap()

    with ExitStack() as ctx:
        def sb(name, shape, dt=F32):
            return ctx.enter_context(nc.sbuf_tensor(name, shape, dt))

        def psum(name, shape):
            return ctx.enter_context(nc.psum_tensor(name, shape, F32))

        def sem(name):
            return ctx.enter_context(nc.semaphore(name))

        resid = sb("resid", [P, NT, D])
        gath = sb("gath", [P, RING, PARTS * D + 2], BF16)
        onehot = [sb(f"onehot{p}", [P, RING, P], BF16) for p in range(2)]
        dst_f = sb("dst_f", [P, GROUP * (2 ** BLOCK_BITS + 1)])
        idx_ring = sb("idx_ring", [P, 2, RING], I32)
        win_blocks = sb("win_blocks", [1, NT // 2], I32)
        w_gnn = sb("w_gnn", [P, KD, 2, 2 * D])
        w_gnn2 = sb("w_gnn2", [P, KD, 2 * D])
        w1_sb = w_gnn[:].rearrange("p k l n -> p k (l n)")
        w2_sb = sb("w2_sb", [P, KH, D])
        bias0 = sb("bias0", [P, KD])
        bias = sb("bias", [P, LAYERS - 1, D])
        b2_sb = sb("b2_sb", [P, D])
        b1_sb = sb("b1_sb", [P, KH])
        wr_sb = sb("wr_sb", [P, D])
        br_sb = sb("br_sb", [P, 1])
        iota_row = sb("iota_row", [P, P])
        iota_col = sb("iota_col", [P, 1])
        window_ids = [sb(f"window_ids{p}", [P, P]) for p in range(2)]
        node_rev = sb("node_rev", [P, NT])
        window_base = sb("window_base", [P, NT])
        ident = sb("ident", [P, P])
        zeros = sb("zeros", [P, 2 * D], BF16)
        ones = sb("ones", [P, P])
        xb = [sb(f"xb{p}", [P, D]) for p in range(2)]
        feat = [sb(f"feat{p}", [P, D]) for p in range(2)]
        x1 = [sb(f"x1_{p}", [P, D]) for p in range(2)]
        featT = [sb(f"featT{p}", [P, KD, P]) for p in range(2)]
        split = [sb(f"split{p}", [P, PARTS, D], BF16) for p in range(2)]
        rest = sb("rest", [P, D])
        hidT = [sb(f"hidT{p}", [P, KH, P]) for p in range(2)]
        yw = [sb(f"yw{p}", [P, D]) for p in range(2)]
        stats4 = [sb(f"stats4_{p}", [P, BATCH, 6]) for p in range(2)]
        mv4 = [sb(f"mv4_{p}", [P, BATCH, 2]) for p in range(2)]
        sd4 = [sb(f"sd4_{p}", [P, BATCH]) for p in range(2)]
        rstd4 = [sb(f"rstd4_{p}", [P, BATCH]) for p in range(2)]
        stats = [sb(f"stats{p}", [P, 6]) for p in range(2)]
        mv = [sb(f"mv{p}", [P, 2]) for p in range(2)]
        sd = [sb(f"sd{p}", [P, 1]) for p in range(2)]
        rstd = [sb(f"rstd{p}", [P, 1]) for p in range(2)]
        eps = sb("eps", [P, 1])
        deg = sb("deg", [P, 1])
        inv_deg = sb("inv_deg", [P, NT])
        weight = sb("weight", [P, NT])
        fin = [area[:, k * BATCH * D:(k + 1) * BATCH * D].rearrange("p (b d) -> p b d", d=D)
               for area, bufs in ((gath[:].rearrange("p r d -> p (r d)").bitcast(F32), 6),
                                  (onehot[0][:].rearrange("p r d -> p (r d)").bitcast(F32), 1),
                                  (onehot[1][:].rearrange("p r d -> p (r d)").bitcast(F32), 1),
                                  (dst_f[:], 2), (w_gnn[:].rearrange("p k l n -> p (k l n)"), 2))
               for k in range(bufs)]
        assert len(fin) == FIN_BUFS
        part = sb("part", [P, TRIALS])
        trial = sb("trial", [P, TRIALS])
        gains = sb("gains", [P, TRIALS])
        sel = sb("sel", [P, NT])

        agg = [psum(f"agg{p}", [P, 2, D]) for p in range(2)]
        agg_lo = [psum(f"agg_lo{p}", [P, 512]) for p in range(2)]
        tp = psum("tp", [P, KD, 256])
        hid = psum("hid", [P, 2, 512])
        y0 = psum("y0", [P, 512])
        yb = [y0[:], hid[:, 0, :]]

        rest4 = [hidT[p][:].rearrange("p k n -> p (k n)").rearrange("p (b d) -> p b d", d=D) for p in range(2)]
        zT = [hidT[p][:, 0:2 * KD, :] for p in range(2)]
        totals_ps = agg_lo[0][:, 0:TRIALS]
        hT = hid[:, 1, 0:KD * P].rearrange("p (k n) -> p k n", k=KD)

        FREE_WINDOWS = 48
        at = [FREE_WINDOWS * D]

        def scratch(cols, dt=F32):
            a = resid[:].rearrange("p n d -> p (n d)")[:, at[0]:at[0] + cols]
            at[0] += cols
            return a if dt == F32 else a.bitcast(dt)

        last_dst = scratch(BLOCKS, I32)
        last_win = scratch(BLOCKS, I32)
        last_winf = scratch(BLOCKS)
        before = scratch(BLOCKS)
        edge_i = scratch(2 * CHUNKS * P, I32).rearrange("p (s c e) -> p s c e", s=2, e=P)
        edge_f = scratch(2 * CHUNKS * P).rearrange("p (s c e) -> p s c e", s=2, e=P)
        idx_all = scratch(CHUNKS * P, I32)
        win_cnt = scratch(1)
        win_block = scratch(NT + 2, I32).rearrange("p (j t) -> p j t", t=2)
        shifted = scratch(NT, I32).rearrange("p (t j) -> p t j", t=2)
        assert at[0] <= LAST_LOOPED * D

        consts = sem("consts")
        w_loaded = sem("w_loaded")
        edges_loaded = sem("edges_loaded")
        last_loaded = sem("last_loaded")
        prep = sem("prep")
        bcast_ready = sem("bcast_ready")
        ends_T = sem("ends_T")
        edge_T = sem("edge_T")
        edge_T_copied = sem("edge_T_copied")
        steps_ready = sem("steps_ready")
        ids_ready = sem("ids_ready")
        lo_added = sem("lo_added")
        mid_added = sem("mid_added")
        idx_stored = sem("idx_stored")
        idx_loaded = [sem(f"idx_loaded{h}") for h in range(2)]
        landed = [sem(f"landed{j}") for j in range(RING)]
        rows_ready = sem("rows_ready")
        slots_free = sem("slots_free")
        pool_turn = sem("pool_turn")
        dve_turn = sem("dve_turn")
        onehot_ready = sem("onehot_ready")
        agg_ready = sem("agg_ready")
        ident_ready = sem("ident_ready")
        x0_loaded = [sem(f"x0_loaded{k}") for k in range(4)]
        pad_ready = sem("pad_ready")
        stats4_ready = sem("stats4_ready")
        mv4_ready = sem("mv4_ready")
        sd4_ready = sem("sd4_ready")
        rstd4_ready = sem("rstd4_ready")
        ln_ready = sem("ln_ready")
        hi4_ready = sem("hi4_ready")
        rest4_ready = sem("rest4_ready")
        mid4_ready = sem("mid4_ready")
        lo4_ready = sem("lo4_ready")
        slots_stored = [sem(f"slots_stored{k}") for k in range(4)]
        mean_ready = sem("mean_ready")
        ln_copied = sem("ln_copied")
        z_tp_ready = sem("z_tp_ready")
        zT_ready = sem("zT_ready")
        hT_ready = sem("hT_ready")
        x_loaded = [sem(f"x_loaded{p}") for p in range(2)]
        stats_ready = sem("stats_ready")
        mv_ready = sem("mv_ready")
        sd_ready = sem("sd_ready")
        rstd_ready = sem("rstd_ready")
        deg_ready = sem("deg_ready")
        inv_ready = sem("inv_ready")
        o_ready = sem("o_ready")
        x1_ready = sem("x1_ready")
        base_ready = sem("base_ready")
        feat_ready = sem("feat_ready")
        tp_ready = sem("tp_ready")
        featT_ready = sem("featT_ready")
        mm_ready = sem("mm_ready")
        hi_ready = sem("hi_ready")
        rest_ready = sem("rest_ready")
        self_ready = sem("self_ready")
        mid_ready = sem("mid_ready")
        lo_ready = sem("lo_ready")
        stored = [sem(f"stored{p}") for p in range(2)]
        w1_loaded = sem("w1_loaded")
        f1_ready = sem("f1_ready")
        gelu_ready = sem("gelu_ready")
        y_ready = sem("y_ready")
        routed_ready = sem("routed_ready")
        route_ready = sem("route_ready")
        weight_ready = sem("weight_ready")
        ysum_ready = sem("ysum_ready")
        yw_ready = sem("yw_ready")
        yw_stored = [sem(f"yw_stored{p}") for p in range(2)]
        sel_step = sem("sel_step")
        part_ready = sem("part_ready")
        total_ready = sem("total_ready")
        fin_loaded = [sem(f"fin_loaded{k}") for k in range(FIN_BUFS)]
        fin_ready = sem("fin_ready")
        fin_stored = [sem(f"fin_stored{k}") for k in range(FIN_BUFS)]

        N_CONSTS = 10
        N_WEIGHTS = 16 * (2 * LAYERS + LAYERS + 5)

        def upto(phase, n):
            return n + ((phase - 1) * NT + 1)

        def turned(phase, n):
            return n + ((phase - 2) * NT + 1)

        def over_windows(eng, depth, slot):
            for w in range(PEEL):
                slot(w, w // 2, w % 2)
            with eng.Fori(PEEL // 2, LAST_LOOPED // 2) as i:
                for p in range(2):
                    slot(i * 2 + p, i, p)
            for w in range(LAST_LOOPED, NT + depth):
                slot(w, w // 2, w % 2)

        def exists(n):
            return not isinstance(n, int) or 0 <= n < NT

        def earlier(half, p, delay):
            return half - (delay - p + 1) // 2

        def col(n):
            return bass.ds(n, 1) if not isinstance(n, int) else slice(n, n + 1)

        def window_rows(t, n):
            return t[n * P:n * P + rows(n), :] if isinstance(n, int) else t[bass.ds(n * P, P), :]

        def pair_blocks(eng):
            found = []

            def first_last(half, p):
                if p == 0:
                    packed = eng.value_load(win_blocks[0:1, col(half)], min_val=0, max_val=2 ** (3 * BLOCK_BITS) - 1)
                    mask = 2 ** BLOCK_BITS - 1
                    found[:] = [eng.snap(value, min_val=0, max_val=BLOCKS - 1) for value in
                                (packed & mask, (packed >> BLOCK_BITS) & mask, packed >> (2 * BLOCK_BITS))]
                return found[p], found[p + 1]
            return first_last

        TURNS = LAST_LOOPED // (FIN_BUFS * BATCH)

        def over_batches(eng, slot, first, last):
            if first == 0:
                for q in range(4):
                    slot(0, q)
                first = 1
            if last > first:
                with eng.Fori(first, min(last, BATCHES // 4)) as turn:
                    for q in range(4):
                        slot(turn, q)
            if last > BATCHES // 4:
                for q in range(4):
                    slot(BATCHES // 4, q)

        def batch(turn, q, delay):
            b = turn * 4 + (q - delay)
            return None if isinstance(b, int) and not 0 <= b < BATCHES else b

        def batch_windows(b):
            n = b * BATCH
            return range(n, NT) if isinstance(b, int) and b == BATCHES - 1 else [n + i for i in range(BATCH)]

        def batch_turn(turn, q, delay, scale):
            return turn * scale + (scale if q >= delay else 0)

        def window_span(t, n):
            return t[bass.ds(n * P, BATCH * P), :].rearrange("(b p) d -> p b d", p=P)

        block = ctx.enter_context(nc.Block())

        @block.sync
        def _(sp):
            def load_x(turn, q):
                b = batch(turn, q, 0)
                if b is None:
                    return
                if not isinstance(turn, int) or turn:
                    sp.wait_ge(x0_loaded[q], turn * 16)
                if isinstance(b, int) and b == BATCHES - 1:
                    sp.wait_ge(pad_ready, 1)
                    for k, n in enumerate(batch_windows(b)):
                        sp.wait_ge(x0_loaded[k], turn * 16)
                        sp.dma_start(resid[0:rows(n), n, :], window_rows(x, n)).then_inc(x0_loaded[k], 16)
                else:
                    sp.dma_start(resid[:, bass.ds(b * BATCH, BATCH), :], window_span(x, b * BATCH)
                                 ).then_inc(x0_loaded[q], 16)
            for q in range(4):
                load_x(0, q)
            whole, done = WHOLE * P * P, (TILES - 1) * P
            sp.wait_ge(consts, N_CONSTS)
            for h, e in enumerate((src, dst)):
                sp.dma_start(edge_i[:, h, 0:WHOLE, :],
                             e[0:whole].rearrange("(c p e) -> p c e", p=P, e=P)).then_inc(edges_loaded, 16)
                sp.dma_start(edge_i[0:TILES - 1 - WHOLE * P, h, WHOLE, :],
                             e[whole:done].rearrange("(t e) -> t e", e=P)).then_inc(edges_loaded, 16)
                row = TILES - 1 - WHOLE * P
                sp.dma_start(edge_i[row:row + 1, h, WHOLE, 0:TAIL_EDGES],
                             e[done:E].rearrange("(t e) -> t e", t=1)).then_inc(edges_loaded, 16)
            with nc.allow_non_contiguous_dma("one destination per block"):
                sp.dma_start(last_dst[0:1, 0:BLOCKS - 1],
                             dst[0:(BLOCKS - 1) * GROUP * P].rearrange("(b e) -> e b", e=GROUP * P)
                             [GROUP * P - 1:GROUP * P, :]).then_inc(last_loaded, 16)
            for l in range(LAYERS):
                w_l = w_gnn[:, :, l, :] if l < 2 else w_gnn2[:]
                for h, w in enumerate((w_neigh[l], w_self[l])):
                    sp.dma_start(w_l[:, :, h * D:(h + 1) * D],
                                 w.rearrange("(k p) n -> p k n", p=P)).then_inc(w_loaded, 16)
                if l:
                    sp.dma_start(bias[:, l - 1, :], b_gnn[l].partition_broadcast(P)).then_inc(w_loaded, 16)
            sp.dma_start(w2_sb[:], w2.rearrange("(k p) n -> p k n", p=P)).then_inc(w_loaded, 16)
            sp.dma_start(b2_sb[:], b2.partition_broadcast(P)).then_inc(w_loaded, 16)
            sp.dma_start(br_sb[:], br.partition_broadcast(P)).then_inc(w_loaded, 16)
            with nc.allow_non_contiguous_dma("small vectors onto the partitions"):
                sp.dma_start(b1_sb[:], b1.rearrange("(k p) -> p k", p=P)).then_inc(w_loaded, 16)
                sp.dma_start(bias0[:], b_gnn[0].rearrange("(k p) -> p k", p=P)).then_inc(w_loaded, 16)
            sp.dma_start(wr_sb[:], wr.rearrange("k o -> (k o)").partition_broadcast(P)).then_inc(w_loaded, 16)

            with sp.Fori(1, FREE_WINDOWS // (4 * BATCH)) as turn:
                for q in range(4):
                    load_x(turn, q)

            sp.wait_ge(steps_ready, 1)
            sp.dma_start(idx_dram[:, 0:PADDED], idx_all[:, 0:PADDED]).then_inc(idx_stored, 16)
            sp.dma_start(idx_dram[:, PADDED:PADDED + 2 * RING], idx_all[:, 0:2 * RING]).then_inc(idx_stored, 16)
            sp.wait_ge(idx_stored, 32)
            for h in range(2):
                sp.dma_start(idx_ring[:, h, :], idx_dram[:, h * RING:(h + 1) * RING]).then_inc(idx_loaded[h], 16)

            over_batches(sp, load_x, FREE_WINDOWS // (4 * BATCH), BATCHES)

            for layer in range(LAYERS):
                with sp.Fori(0, TURNS_PER_LAYER) as it:
                    for h in range(2):
                        for j in range(RING):
                            sp.wait_ge(landed[j], it * 32 + 16 * (2 * layer * TURNS_PER_LAYER + h + 1))
                            if j % GROUP == GROUP - 1:
                                sp.sem_inc(rows_ready, 1)
                        sp.dma_start(idx_ring[:, h, :],
                                     idx_dram[:, bass.ds(it * TURN_TILES + (h + 2) * RING, RING)]
                                     ).then_inc(idx_loaded[h], 16)
            for h in range(2):
                sp.wait_ge(idx_loaded[h], 16 * (LAYERS * TURNS_PER_LAYER + 1))

            sp.wait_ge(agg_ready, NT * LAYERS)
            for p in range(2):
                sp.wait_ge(yw_stored[p], 16 * (FIN_BUFS * BATCH // 2))

            def load_batch(it, k):
                sp.dma_start(fin[k], window_span(yw_dram, it * (FIN_BUFS * BATCH) + k * BATCH)
                             ).then_inc(fin_loaded[k], 16)
            for k in range(FIN_BUFS):
                if k == FIN_BUFS - 2:
                    sp.wait_ge(f1_ready, NT)
                load_batch(0, k)
            for p in range(2):
                sp.wait_ge(yw_stored[p], 16 * (NT // 2))
            with sp.Fori(1, TURNS) as it:
                for k in range(FIN_BUFS):
                    sp.wait_ge(fin_stored[k], it * 16)
                    load_batch(it, k)
            for p, n in enumerate(range(LAST_LOOPED, NT)):
                sp.wait_ge(fin_stored[p], 16 * TURNS)
                sp.dma_start(fin[p][0:rows(n), 0, :], window_rows(yw_dram, n)).then_inc(fin_loaded[p], 16)

        @block.gpsimd
        def _(pool):
            g = nc.gpsimd
            small = dict(allow_small_or_imprecise_dtypes=True)
            g.iota(iota_row[:], [[1, P]], base=0, channel_multiplier=0, **small).then_inc(consts, 1)
            g.iota(iota_col[:], [[1, 1]], base=0, channel_multiplier=1, **small).then_inc(consts, 1)
            g.iota(window_base[:], [[P, NT]], base=0, channel_multiplier=0, **small).then_inc(consts, 1)
            g.iota(node_rev[:], [[-P, NT]], base=N, channel_multiplier=-1, **small).then_inc(consts, 1)

            def batch_tiles(b, q, delay):
                cols, k = len(batch_windows(b)), (q - delay) % 4
                return cols, resid[:, bass.ds(b * BATCH, cols), :], gath[:, k * BATCH:k * BATCH + cols, :]

            def first_rest(turn, q):
                b, p = batch(turn, q, 2), q % 2
                if b is None:
                    return
                cols, ln, parts = batch_tiles(b, q, 2)
                pool.wait_ge(hi4_ready, turn * 4 + (q - 1))
                if not isinstance(b, int) or b >= 2:
                    pool.wait_ge(lo4_ready, turn * 4 + (q - 3))
                g.tensor_tensor(rest4[p][:, 0:cols, :], ln, parts[:, :, 0:D], ALU.subtract).then_inc(rest4_ready, 1)

            def last_part(turn, q):
                b, p = batch(turn, q, 3), 1 - q % 2
                if b is None:
                    return
                cols, ln, parts = batch_tiles(b, q, 3)
                pool.wait_ge(mid4_ready, turn * 4 + (q - 2))
                g.tensor_tensor(parts[:, :, 2 * D:3 * D], rest4[p][:, 0:cols, :], parts[:, :, D:2 * D],
                                ALU.subtract).then_inc(lo4_ready, 1)

            def slot_phase0(turn, q):
                first_rest(turn, q)
                last_part(turn, q)
            over_batches(pool, slot_phase0, 0, BATCHES)

            for layer in range(LAYERS):
                if layer:
                    for p in range(2):
                        pool.wait_ge(stored[p], 16 * (NT // 2) * layer)
                else:
                    for k in range(4):
                        pool.wait_ge(slots_stored[k], 16 * (1 + BATCHES // 4 + (k < 2)))
                with pool.Fori(0, TURNS_PER_LAYER) as it:
                    for h in range(2):
                        pool.wait_ge(idx_loaded[h], it * 16 + 16 * (layer * TURNS_PER_LAYER + 1))
                        for q in range(RING_BLOCKS):
                            pool.wait_ge(slots_free, it * (2 * RING_BLOCKS)
                                         + (layer * PADDED_BLOCKS + h * RING_BLOCKS + q + 1))
                            pool.sem_inc(pool_turn, 1)
                            for j in range(q * GROUP, (q + 1) * GROUP):
                                g.indirect_dma_start(gath[:, j, 0:PARTS * D], None, table[layer][:, :],
                                                     bass.IndirectOffsetOnAxis(ap=idx_ring[:, h, j:j + 1], axis=0)
                                                     ).then_inc(landed[j], 16)

        @block.tensor
        def _(pe):
            mm = nc.tensor.matmul
            pe.sem_inc(slots_free, RING_BLOCKS)
            pe.wait_ge(consts, N_CONSTS)
            pe.wait_ge(ident_ready, 1)

            pe.wait_ge(prep, 3)
            mm(y0[:, 0:BLOCKS - 1], ones[0:1, :], last_winf[0:1, 0:BLOCKS - 1], start=True, stop=True
               ).then_inc(bcast_ready, 1)
            pe.wait_ge(prep, 5)
            nc.tensor.transpose(tp[0:1, 0, 0:P], win_cnt, ident[:]).then_inc(ends_T, 1)
            pe.wait_ge(prep, 8)
            for c in range(CHUNKS):
                for h in range(2):
                    pe.wait_ge(edge_T_copied, c * 2 + (h + 1))
                    nc.tensor.transpose(yb[h][:, 0:P], edge_f[:, h, c, :], ident[:]).then_inc(edge_T, 1)
            pe.wait_ge(w_loaded, N_WEIGHTS)
            pe.wait_ge(edge_T_copied, CHUNKS * 2 + 2)

            def transposes(phase, n, p):
                pe.wait_ge(feat_ready, turned(phase, n))
                if phase == 2 and isinstance(n, int) and n == 0:
                    pe.wait_ge(zT_ready, NT)
                else:
                    pe.wait_ge(featT_ready, upto(phase, n - 1))
                r = rows(n)
                for k in range(KD):
                    last = nc.tensor.transpose(tp[:, k, 0:r], feat[p][0:r, k * P:(k + 1) * P], ident[0:r, 0:r])
                last.then_inc(tp_ready, 1)

            def layer_product(phase, n, p):
                pe.wait_ge(featT_ready, upto(phase, n))
                if phase > 1 or not isinstance(n, int) or n >= 2:
                    pe.wait_ge(lo_ready, upto(phase, n - 2))
                r = rows(n)
                for k in range(KD):
                    w = w_gnn[:, k, phase, :] if phase < 2 else w_gnn2[:, k, :]
                    last = mm(yb[p][0:r, :], featT[p][:, k, 0:r], w, start=(k == 0), stop=(k == KD - 1))
                last.then_inc(mm_ready, 1)

            def transposes_z(n, p):
                pe.wait_ge(mean_ready, n + 1)
                pe.wait_ge(ln_copied, n + 1)
                if not isinstance(n, int) or n:
                    pe.wait_ge(zT_ready, n)
                r = rows(n)
                for k in range(KD):
                    for h, z in enumerate((feat[p], xb[p])):
                        last = nc.tensor.transpose(tp[:, h, k * P:k * P + r], z[0:r, k * P:(k + 1) * P],
                                                   ident[0:r, 0:r])
                last.then_inc(z_tp_ready, 1)

            def product0(n, p):
                pe.wait_ge(zT_ready, n + 1)
                if not isinstance(n, int) or n:
                    pe.wait_ge(featT_ready, n)
                r = rows(n)
                for m in range(KD):
                    for k in range(2 * KD):
                        h = k // KD
                        last = mm(hT[:, m, 0:r], w_gnn[:, k % KD, 0, h * D + m * P:h * D + (m + 1) * P],
                                  zT[p][:, k, 0:r], start=(k == 0), stop=(k == 2 * KD - 1))
                last.then_inc(hT_ready, 1)

            pe_blocks = pair_blocks(pe)

            def aggregate(layer, n, half, p):
                first, shared = pe_blocks(half, p)
                if layer == 2 and (not isinstance(n, int) or n >= 2):
                    pe.wait_ge(o_ready, n - 1)
                elif layer == 2:
                    pe.wait_ge(feat_ready, turned(2, NT - 2 + n))
                elif layer == 1 and (not isinstance(n, int) or n >= 2):
                    pe.wait_ge(feat_ready, turned(2, n - 2))
                elif layer == 1:
                    pe.wait_ge(mean_ready, NT - 2 + n + 1)
                elif not isinstance(n, int) or n >= 2:
                    pe.wait_ge(mean_ready, n - 1)
                lo_cols = D + 1 if layer == 0 else D
                hi_mid = agg[p][:].rearrange("p a d -> p (a d)")
                free = dict(stop=False, skip_group_check=True)
                ends = dict(stop=True, skip_group_check=True)
                mm(hi_mid, zeros[:, 0:P], zeros[:, 0:2 * D], start=True, **free)
                mm(agg_lo[p][:, 0:lo_cols], zeros[:, 0:P], zeros[:, 0:lo_cols], start=True, **free)

                def block_products(b, last_block=False):
                    base = pe.snap((b % RING_BLOCKS) * GROUP)
                    pe.wait_ge(onehot_ready, b + n + (layer * PAIRS + 1))
                    pe.wait_ge(rows_ready, b + (layer * PADDED_BLOCKS + 1))
                    for j in range(GROUP):
                        oh = onehot[p][:, bass.ds(base, GROUP), :][:, j:j + 1, :]
                        tile_rows = gath[:, bass.ds(base, GROUP), :][:, j:j + 1, :]
                        flags = ends if last_block and j == GROUP - 1 else free
                        mm(hi_mid, oh, tile_rows[:, :, 0:2 * D], start=False, **flags)
                        last = mm(agg_lo[p][:, 0:lo_cols], oh, tile_rows[:, :, 2 * D:2 * D + lo_cols],
                                  start=False, **flags)
                    return last
                with pe.If(first < shared):
                    with pe.Fori(first, shared) as b:
                        block_products(b).then_inc(slots_free, 1)
                block_products(shared, last_block=True).then_inc(agg_ready, 1)
                if isinstance(n, int) and n == NT - 1:
                    pe.wait_ge(rows_ready, (layer + 1) * PADDED_BLOCKS)
                    pe.wait_ge(agg_ready, (layer + 1) * NT)
                    pe.sem_inc(slots_free, PADDED_BLOCKS - BLOCKS + 1)

            pe.wait_ge(steps_ready, 1)

            def slot_layer0(w, half, p):
                if exists(w - 4):
                    layer_product(1, w - 4, p)
                if exists(w - 3):
                    product0(w - 3, 1 - p)
                if exists(w - 2):
                    transposes_z(w - 2, p)
                if exists(w):
                    aggregate(0, w, half, p)
            over_windows(pe, 4, slot_layer0)

            def slot_layer1(w, half, p):
                if exists(w - 3):
                    layer_product(2, w - 3, 1 - p)
                if exists(w - 2):
                    transposes(2, w - 2, p)
                if exists(w):
                    aggregate(1, w, half, p)
            over_windows(pe, 3, slot_layer1)

            def ffn_up(n, p):
                pe.wait_ge(featT_ready, upto(3, n))
                if not isinstance(n, int) or n:
                    pe.wait_ge(gelu_ready, n)
                r = rows(n)
                for j in range(KH):
                    for k in range(KD):
                        last = mm(hid[:, j // 4, (j % 4) * P:(j % 4) * P + r], w1_sb[:, k, j * P:(j + 1) * P],
                                  featT[p][:, k, 0:r], start=(k == 0), stop=(k == KD - 1))
                last.then_inc(f1_ready, 1)

            def ffn_down(n, p):
                pe.wait_ge(gelu_ready, n + 1)
                if not isinstance(n, int) or n:
                    pe.wait_ge(yw_ready, n)
                r = rows(n)
                for j in range(KH):
                    last = mm(y0[0:r, 0:D], hidT[p][:, j, 0:r], w2_sb[:, j, :], start=(j == 0), stop=(j == KH - 1))
                last.then_inc(y_ready, 1)

            pe.wait_ge(w1_loaded, 16)
            pe.wait_ge(lo_ready, upto(2, NT - 1))

            def slot_ffn(w, half, p):
                if exists(w - 2):
                    transposes(3, w - 2, p)
                if exists(w - 4):
                    ffn_down(w - 4, p)
                if exists(w - 3):
                    ffn_up(w - 3, 1 - p)
                if exists(w):
                    aggregate(2, w, half, p)
            over_windows(pe, 1, slot_ffn)

            def total(i):
                pe.wait_ge(part_ready, i + 1)
                mm(totals_ps, ones[:], part[:], start=True, stop=True).then_inc(total_ready, 1)

            last = NT - 1
            total(0)
            transposes(3, last, last % 2)
            ffn_down(last - 2, last % 2)
            total(1)
            ffn_up(last - 1, 1 - last % 2)
            total(2)
            ffn_down(last - 1, 1 - last % 2)
            total(3)
            ffn_up(last, last % 2)
            total(4)
            ffn_down(last, last % 2)
            total(5)
            with pe.Fori(FFN_ROUNDS, sum(ROUNDS) + 2) as i:
                total(i)

        @block.vector
        def _(dve):
            v = nc.vector
            v.memset(zeros[:], 0.0).then_inc(consts, 1)
            v.memset(ones[:], 1.0).then_inc(consts, 1)
            v.memset(eps[:], LN_EPS).then_inc(consts, 1)
            v.memset(gath[:, :, PARTS * D:PARTS * D + 2], 1.0).then_inc(consts, 1)
            v.memset(edge_i[:, 0, WHOLE:CHUNKS, :], 0).then_inc(consts, 1)
            v.memset(edge_i[:, 1, WHOLE:CHUNKS, :], N).then_inc(consts, 1)
            dve.wait_ge(consts, N_CONSTS)
            v.tensor_scalar(ident[:], iota_row[:], iota_col[:, 0:1], None, ALU.is_equal).then_inc(ident_ready, 1)

            def statistics(turn, q):
                b, p = batch(turn, q, 0), q % 2
                if b is None:
                    return
                done = turn * 4 + (q + 1)
                last = isinstance(b, int) and b == BATCHES - 1
                for k in range(2 if last else 1):
                    dve.wait_ge(x0_loaded[q + k], turn * 16 + 16)
                if not isinstance(b, int) or b >= 2:
                    dve.wait_ge(ln_ready, turn * 4 + (q - 1))
                for i, n in enumerate(batch_windows(b)):
                    ins = v.bn_stats(stats4[p][:, i, :], resid[:, col(n), :].rearrange("p n d -> p (n d)"))
                ins.then_inc(stats4_ready, 1)
                dve.wait_ge(stats4_ready, done)
                dve.sem_inc(dve_turn, 1)
                for i, n in enumerate(batch_windows(b)):
                    ins = v.bn_aggr(mv4[p][:, i, :], stats4[p][:, i, :])
                ins.then_inc(mv4_ready, 1)

            def normalise4(turn, q):
                b, p = batch(turn, q, 1), 1 - q % 2
                if b is None:
                    return
                done = turn * 4 + q
                dve.wait_ge(sd4_ready, done)
                cols = len(batch_windows(b))
                v.reciprocal(rstd4[p][:, 0:cols], sd4[p][:, 0:cols]).then_inc(rstd4_ready, 1)
                dve.wait_ge(rstd4_ready, done)
                for i, n in enumerate(batch_windows(b)):
                    ins = v.tensor_scalar(resid[:, col(n), :], resid[:, col(n), :], mv4[p][:, i, 0:1],
                                          rstd4[p][:, i:i + 1], ALU.subtract, ALU.mult)
                ins.then_inc(ln_ready, 1)

            def slot_phase0(turn, q):
                statistics(turn, q)
                normalise4(turn, q)
            PREP_TURN = 1
            over_batches(dve, slot_phase0, 0, PREP_TURN)

            v.memset(win_block[0:1, 0, 0:1], 0).then_inc(prep, 1)
            dve.wait_ge(last_loaded, 16)
            v.tensor_scalar(last_win[0:1, 0:BLOCKS - 1], last_dst[0:1, 0:BLOCKS - 1], P.bit_length() - 1, None,
                            ALU.arith_shift_right).then_inc(prep, 1)
            dve.wait_ge(prep, 2)
            v.tensor_copy(last_winf[0:1, 0:BLOCKS - 1], last_win[0:1, 0:BLOCKS - 1]).then_inc(prep, 1)
            dve.wait_ge(bcast_ready, 1)
            v.tensor_scalar(before[:, 0:BLOCKS - 1], y0[:, 0:BLOCKS - 1], iota_col[:, 0:1], None,
                            ALU.is_le).then_inc(prep, 1)
            dve.wait_ge(prep, 4)
            v.tensor_reduce(win_cnt, before[:, 0:BLOCKS - 1], AX.X, ALU.add).then_inc(prep, 1)
            dve.wait_ge(ends_T, 1)
            v.tensor_copy(win_block[0:1, :, :].rearrange("p j t -> p (j t)")[:, 1:NT + 1], tp[0:1, 0, 0:NT]
                          ).then_inc(prep, 1)
            dve.wait_ge(edges_loaded, 6 * 16)
            for h in range(2):
                v.tensor_copy(edge_f[:, h, :, :], edge_i[:, h, :, :]).then_inc(prep, 1)
            dve.sem_inc(edge_T_copied, 2)
            with dve.Fori(0, CHUNKS) as c:
                at_c = dve.snap(c * P)
                dve.wait_ge(edge_T, c * 2 + 1)
                v.tensor_copy(idx_all[:, bass.ds(at_c, P)], yb[0][:, 0:P]).then_inc(edge_T_copied, 1)
                dve.wait_ge(edge_T, c * 2 + 2)
                v.tensor_copy(dst_f[:, bass.ds(at_c, P)], yb[1][:, 0:P]).then_inc(edge_T_copied, 1)
            dve.wait_ge(edge_T_copied, 2 * CHUNKS + 2)
            v.memset(weight[:], 0.0).then_inc(prep, 1)
            dve.wait_ge(prep, 9)
            half = NT // 2
            v.tensor_scalar(shifted[0:1, 0, :], win_block[0:1, 0:half, 1], BLOCK_BITS, None,
                            ALU.logical_shift_left).then_inc(prep, 1)
            v.tensor_scalar(shifted[0:1, 1, :], win_block[0:1, 1:half + 1, 0], 2 * BLOCK_BITS, None,
                            ALU.logical_shift_left).then_inc(prep, 1)
            dve.wait_ge(prep, 11)
            v.tensor_tensor(shifted[0:1, 0, :], shifted[0:1, 0, :], shifted[0:1, 1, :],
                            ALU.bitwise_or).then_inc(prep, 1)
            dve.wait_ge(prep, 12)
            v.tensor_tensor(win_blocks[0:1, :], shifted[0:1, 0, :], win_block[0:1, 0:half, 0],
                            ALU.bitwise_or).then_inc(prep, 1)
            dve.wait_ge(prep, 13)
            dve.sem_inc(steps_ready, 1)
            v.memset(resid[:, LAST_LOOPED:NT, :], 0.0).then_inc(pad_ready, 1)
            dve.wait_ge(pad_ready, 1)
            over_batches(dve, slot_phase0, PREP_TURN, BATCHES)
            dve.wait_ge(w_loaded, N_WEIGHTS)
            dve.wait_ge(lo4_ready, BATCHES)

            def x_stats(n, p, src_tile):
                v.bn_stats(stats[p][0:rows(n), :], src_tile).then_inc(stats_ready, 1)
                dve.wait_ge(stats_ready, n + 1)
                dve.sem_inc(dve_turn, 1)
                v.bn_aggr(mv[p][0:rows(n), :], stats[p][0:rows(n), :]).then_inc(mv_ready, 1)

            def normalise(phase, n, p, src_tile):
                r = rows(n)
                at_n = n + 1
                dve.wait_ge(sd_ready, at_n)
                v.reciprocal(rstd[p][0:r, :], sd[p][0:r, :]).then_inc(rstd_ready, 1)
                dve.wait_ge(rstd_ready, at_n)
                dve.wait_ge(tp_ready, turned(phase, n - 2))
                v.tensor_scalar(feat[p][0:r, :], src_tile, mv[p][0:r, 0:1], rstd[p][0:r, 0:1],
                                ALU.subtract, ALU.mult).then_inc(feat_ready, 1)

            def split_product(phase, n, p):
                r = rows(n)
                dve.wait_ge(mm_ready, upto(phase, n))
                dve.wait_ge(hi_ready, upto(phase, n))
                if phase > 1 or not isinstance(n, int) or n:
                    dve.wait_ge(lo_ready, upto(phase, n - 1))
                v.tensor_tensor(rest[0:r, :], yb[p][0:r, 0:D], split[p][0:r, 0, :],
                                ALU.subtract).then_inc(rest_ready, 1)
                v.tensor_tensor(resid[0:r, col(n), :], yb[p][0:r, D:2 * D], bias[0:r, phase - 1, :],
                                ALU.add).then_inc(self_ready, 1)
                dve.wait_ge(mid_ready, upto(phase, n))
                v.tensor_tensor(split[p][0:r, 2, :], rest[0:r, :], split[p][0:r, 1, :],
                                ALU.subtract).then_inc(lo_ready, 1)

            dve_blocks = pair_blocks(dve)

            def onehots(layer, n, half, p):
                first, shared = dve_blocks(half, p)
                v.tensor_scalar(window_ids[p][:], iota_row[:], window_base[:, col(n)], None,
                                ALU.add).then_inc(ids_ready, 1)
                dve.wait_ge(ids_ready, n + (layer * NT + 1))
                dve.sem_inc(dve_turn, 1)

                def block_onehots(b):
                    slot, tiles = dve.snap((b % RING_BLOCKS) * GROUP), dve.snap(b * GROUP)
                    dve.wait_ge(slots_free, b + (layer * PADDED_BLOCKS + 1))
                    v.tensor_tensor(onehot[p][:, bass.ds(slot, GROUP), :],
                                    window_ids[p][:].unsqueeze(1).to_broadcast([P, GROUP, P]),
                                    dst_f[:, bass.ds(tiles, GROUP)].unsqueeze(2).to_broadcast([P, GROUP, P]),
                                    ALU.is_equal).then_inc(onehot_ready, 1)
                with dve.Fori(first, shared + 1) as b:
                    block_onehots(b)

            def mean_done(n, p):
                r = rows(n)
                dve.wait_ge(agg_ready, n + 1)
                v.tensor_scalar(deg[0:r, :], agg_lo[p][0:r, D:D + 1], 1.0, None, ALU.max).then_inc(deg_ready, 1)
                dve.wait_ge(deg_ready, n + 1)
                v.reciprocal(inv_deg[0:r, col(n)], deg[0:r, :]).then_inc(inv_ready, 1)
                dve.wait_ge(inv_ready, n + 1)
                if not isinstance(n, int) or n >= 2:
                    dve.wait_ge(z_tp_ready, n - 1)
                mean, inv = feat[p][0:r, :], inv_deg[0:r, col(n)]
                v.tensor_scalar(mean, agg_lo[p][0:r, 0:D], inv, None, ALU.mult).then_inc(lo_added, 1)
                dve.wait_ge(lo_added, n + 1)
                v.scalar_tensor_tensor(out=mean, in0=agg[p][0:r, 1, :], scalar=inv, in1=mean, op0=ALU.mult,
                                       op1=ALU.add).then_inc(mid_added, 1)
                dve.wait_ge(mid_added, n + 1)
                v.scalar_tensor_tensor(out=mean, in0=agg[p][0:r, 0, :], scalar=inv, in1=mean, op0=ALU.mult,
                                       op1=ALU.add).then_inc(mean_ready, 1)

            def aggregate_done(layer, n, p):
                r = rows(n)
                dve.wait_ge(agg_ready, n + (layer * NT + 1))
                total, inv = resid[0:r, col(n), :], inv_deg[0:r, col(n)]
                for sums, added in ((agg_lo[p][0:r, 0:D], lo_added), (agg[p][0:r, 1, :], mid_added)):
                    v.scalar_tensor_tensor(out=total, in0=sums, scalar=inv, in1=total, op0=ALU.mult,
                                           op1=ALU.add).then_inc(added, 1)
                    dve.wait_ge(added, n + (layer * NT + 1))
                o = feat[p] if layer < 2 else rest
                if layer == 1 and (not isinstance(n, int) or n >= 2):
                    dve.wait_ge(tp_ready, turned(2, n - 2))
                elif layer == 1:
                    dve.wait_ge(z_tp_ready, NT)
                v.scalar_tensor_tensor(out=o[0:r, :], in0=agg[p][0:r, 0, :], scalar=inv, in1=total,
                                       op0=ALU.mult, op1=ALU.add
                                       ).then_inc(feat_ready if layer < 2 else o_ready, 1)

            def slot_layer0(w, half, p):
                if exists(w):
                    onehots(0, w, half, p)
                if exists(w - 1):
                    mean_done(w - 1, 1 - p)
                if exists(w - 4):
                    split_product(1, w - 4, p)
            over_windows(dve, 4, slot_layer0)

            dve.wait_ge(self_ready, NT)

            def slot_layer1(w, half, p):
                if exists(w):
                    onehots(1, w, half, p)
                if exists(w - 1):
                    aggregate_done(1, w - 1, 1 - p)
                if exists(w - 3):
                    split_product(2, w - 3, 1 - p)
            over_windows(dve, 3, slot_layer1)

            dve.wait_ge(self_ready, NT * 2)
            dve.wait_ge(lo_ready, NT * 2)

            def ffn_result(n, half, p):
                r = rows(n)
                dve.wait_ge(y_ready, n + 1)
                if not isinstance(n, int) or n >= 2:
                    dve.wait_ge(yw_stored[p], half * 16)
                v.tensor_tensor(yw[p][0:r, :], y0[0:r, 0:D], b2_sb[0:r, :], ALU.add).then_inc(ysum_ready, 1)
                dve.wait_ge(weight_ready, n + 1)
                dve.wait_ge(ysum_ready, n + 1)
                v.tensor_scalar(yw[p][0:r, :], yw[p][0:r, :], weight[0:r, col(n)], None,
                                ALU.mult).then_inc(yw_ready, 1)

            def slot_ffn(w, half, p):
                if exists(w):
                    onehots(2, w, half, p)
                if exists(w - 1):
                    n, q = w - 1, 1 - p
                    r = rows(n)
                    if not isinstance(n, int) or n:
                        dve.wait_ge(route_ready, n)
                    if not isinstance(n, int) or n >= 2:
                        dve.wait_ge(base_ready, n - 1)
                    aggregate_done(2, n, q)
                    dve.wait_ge(x_loaded[q], earlier(half, p, 1) * 16 + 16)
                    dve.wait_ge(o_ready, n + 1)
                    v.tensor_tensor(x1[q][0:r, :], rest[0:r, :], xb[q][0:r, :], ALU.add).then_inc(x1_ready, 1)
                    dve.wait_ge(x1_ready, n + 1)
                    x_stats(n, q, x1[q][0:r, :])
                    normalise(3, n, q, x1[q][0:r, :])
                    dve.wait_ge(feat_ready, turned(3, n))
                    v.tensor_tensor(rest[0:r, :], feat[q][0:r, :], wr_sb[0:r, :], ALU.mult).then_inc(routed_ready, 1)
                    v.tensor_tensor(resid[0:r, col(n), :], x1[q][0:r, :], feat[q][0:r, :],
                                    ALU.add).then_inc(base_ready, 1)
                    dve.wait_ge(routed_ready, n + 1)
                    v.tensor_reduce(weight[0:r, col(n)], rest[0:r, :], AX.X, ALU.add).then_inc(route_ready, 1)
                    dve.wait_ge(route_ready, n + 1)
                    v.tensor_scalar(weight[0:r, col(n)], weight[0:r, col(n)], br_sb[0:r, 0:1], None,
                                    ALU.add).then_inc(weight_ready, 1)
                if exists(w - 4) and not (isinstance(w, int) and w == NT):
                    ffn_result(w - 4, earlier(half, p, 4), p)
            over_windows(dve, 1, slot_ffn)

            key, hi16, lo16 = (x1[0][:, 0:NT].bitcast(I32), x1[1][:, 0:NT].bitcast(I32), xb[0][:, 0:NT].bitcast(I32))
            low, exist = xb[1][:, 0:NT], rest[:, 0:NT]
            cand, flag = (split[p][:].rearrange("p t d -> p (t d)").bitcast(F32)[:, 0:NT] for p in range(2))
            flags = w_gnn2[:].rearrange("p k n -> p (k n)")[:, 0:TRIALS * NT].rearrange("p (t n) -> p t n", n=NT)
            for p in range(2):
                dve.wait_ge(stored[p], 16 * NT)
            st = stats[0]
            thr, step, wanted, gain = (st[:, i:i + 1] for i in range(4))
            count = [0]

            def link(ins, base=0):
                count[0] += 1
                ins.then_inc(sel_step, 1)
                dve.wait_ge(sel_step, base + count[0])

            dve.wait_ge(weight_ready, NT)
            dve.wait_ge(base_ready, NT)
            bits = weight[:].bitcast(I32)
            link(v.tensor_scalar(key, bits, 31, 0x7FFFFFFF, ALU.arith_shift_right, ALU.bitwise_and))
            link(v.tensor_tensor(key, key, bits, ALU.bitwise_xor))
            link(v.tensor_scalar(hi16, key, 16, None, ALU.arith_shift_right))
            link(v.tensor_scalar(lo16, key, 0xFFFF, None, ALU.bitwise_and))
            link(v.tensor_copy(cand, hi16))
            link(v.tensor_copy(low, lo16))
            link(v.tensor_scalar(exist, node_rev[:], 0.5, None, ALU.is_ge))
            link(v.tensor_scalar(cand, cand, float(2 ** 15 + 1), None, ALU.add))
            link(v.tensor_tensor(cand, cand, exist, ALU.mult))
            link(v.memset(sel[:], 0.0))
            link(v.memset(wanted, float(SELECTED)))
            link(v.memset(part[:], 0.0))
            totals = [0]

            def total_of(done):
                v.tensor_reduce(part[:, 0:1], flag, AX.X, ALU.add).then_inc(part_ready, 1)
                dve.wait_ge(total_ready, done + 1)

            def search(rounds, beside=None):
                link(v.memset(thr, 0.0))
                link(v.memset(step, float(2 ** (DIGIT * (rounds - 1)))))
                before, done = count[0], totals[0]
                PER_ROUND = 6

                def one_round(i, base):
                    link(v.tensor_scalar(trial[:], iota_row[:, 1:TRIALS + 1], step, thr, ALU.mult, ALU.add), base)
                    link(v.tensor_tensor(flags, cand.unsqueeze(1).to_broadcast([P, TRIALS, NT]),
                                         trial[:].unsqueeze(2).to_broadcast([P, TRIALS, NT]), ALU.is_ge), base)
                    v.tensor_reduce(part[:], flags, AX.X, ALU.add).then_inc(part_ready, 1)
                    dve.wait_ge(total_ready, i + (done + 1))
                    link(v.tensor_scalar(gains[:], totals_ps, wanted, step, ALU.is_ge, ALU.mult), base)
                    link(v.tensor_reduce(gain, gains[:], AX.X, ALU.add), base)
                    link(v.tensor_tensor(thr, thr, gain, ALU.add), base)
                    link(v.tensor_scalar(step, step, 1.0 / 2 ** DIGIT, None, ALU.mult), base)

                if beside:
                    for i in range(rounds):
                        one_round(i, 0)
                        if i in beside:
                            n = beside[i]
                            ffn_result(n, n // 2, n % 2)
                else:
                    with dve.Fori(0, rounds) as i:
                        count[0] = 0
                        one_round(i, i * PER_ROUND + before)
                        assert count[0] == PER_ROUND
                count[0] = before + PER_ROUND * rounds
                totals[0] += rounds

            for rank, lower in enumerate((low, node_rev[:], None)):
                if rank == 0:
                    ffn_result(NT - 4, NT // 2 - 2, 0)
                    search(ROUNDS[0], beside={1: NT - 3, 3: NT - 2, 5: NT - 1})
                else:
                    search(ROUNDS[rank])
                if lower is None:
                    link(v.tensor_scalar(flag, cand, thr, None, ALU.is_ge))
                    link(v.tensor_tensor(sel[:], sel[:], flag, ALU.add))
                    break
                link(v.tensor_scalar(flag, cand, thr, None, ALU.is_gt))
                link(v.tensor_tensor(sel[:], sel[:], flag, ALU.add))
                total_of(totals[0])
                totals[0] += 1
                link(v.tensor_tensor(wanted, wanted, totals_ps[:, 0:1], ALU.subtract))
                link(v.tensor_scalar(flag, cand, thr, None, ALU.is_equal))
                if rank == 0:
                    link(v.tensor_scalar(cand, lower, 1.0, None, ALU.add))
                    link(v.tensor_tensor(cand, cand, flag, ALU.mult))
                else:
                    link(v.tensor_tensor(cand, lower, flag, ALU.mult))
            assert totals[0] == sum(ROUNDS) + 2

            def add_batch(it, k):
                for b in range(BATCH):
                    n = it * (FIN_BUFS * BATCH) + (k * BATCH + b)
                    last = v.scalar_tensor_tensor(out=fin[k][:, b, :], in0=fin[k][:, b, :], scalar=sel[:, col(n)],
                                                  in1=resid[:, col(n), :], op0=ALU.mult, op1=ALU.add)
                last.then_inc(fin_ready, 1)
            with dve.Fori(0, TURNS) as it:
                for k in range(FIN_BUFS):
                    dve.wait_ge(fin_loaded[k], it * 16 + 16)
                    add_batch(it, k)
            for p, n in enumerate(range(LAST_LOOPED, NT)):
                r = rows(n)
                dve.wait_ge(fin_loaded[p], 16 * (TURNS + 1))
                v.scalar_tensor_tensor(out=fin[p][0:r, 0, :], in0=fin[p][0:r, 0, :], scalar=sel[0:r, n:n + 1],
                                       in1=resid[0:r, n, :], op0=ALU.mult, op1=ALU.add).then_inc(fin_ready, 1)

        @block.scalar
        def _(act):
            a = nc.scalar
            act.wait_ge(consts, N_CONSTS)

            def std_dev(phase, n, p):
                r = rows(n)
                act.wait_ge(mv_ready, n + 1)
                a.activation(sd[p][0:r, :], mv[p][0:r, 1:2], ACT.Sqrt, bias=eps[0:r, 0:1]).then_inc(sd_ready, 1)

            def copy_transposed(phase, n, p):
                r = rows(n)
                act.wait_ge(tp_ready, turned(phase, n))
                if phase == 3 and (not isinstance(n, int) or n >= 2):
                    act.wait_ge(y_ready, n - 1)
                elif phase == 3:
                    act.wait_ge(mm_ready, NT * 2)
                else:
                    act.wait_ge(mm_ready, upto(phase, n - 2))
                func = ACT.Relu if phase == 2 else ACT.Copy
                a.activation(featT[p][:, :, 0:r], tp[:, :, 0:r], func).then_inc(featT_ready, 1)

            def split_store(phase, n, half, p):
                r = rows(n)
                act.wait_ge(mm_ready, upto(phase, n))
                if phase > 1 or not isinstance(n, int) or n >= 2:
                    act.wait_ge(stored[p], half * 16 + 16 * (phase - 1) * (NT // 2))
                a.copy(split[p][0:r, 0, :], yb[p][0:r, 0:D]).then_inc(hi_ready, 1)
                act.wait_ge(rest_ready, upto(phase, n))
                a.copy(split[p][0:r, 1, :], rest[0:r, :]).then_inc(mid_ready, 1)
                act.wait_ge(mid_ready, upto(phase, n))
                act.wait_ge(lo_ready, upto(phase, n))
                act.dma_start(window_rows(table[phase], n),
                              split[p][0:r, :, :].rearrange("p t d -> p (t d)")).then_inc(stored[p], 16)

            def slot_phase0(turn, q):
                b, p = batch(turn, q, 0), q % 2
                if b is not None:
                    cols = len(batch_windows(b))
                    act.wait_ge(mv4_ready, turn * 4 + (q + 1))
                    a.activation(sd4[p][:, 0:cols], mv4[p][:, 0:cols, 1], ACT.Sqrt, bias=eps[:, 0:1]
                                 ).then_inc(sd4_ready, 1)
                b = batch(turn, q, 2)
                if b is not None:
                    cols, k = len(batch_windows(b)), (q - 2) % 4
                    act.wait_ge(rest4_ready, turn * 4 + (q - 1))
                    a.copy(gath[:, k * BATCH:k * BATCH + cols, D:2 * D], rest4[p][:, 0:cols, :]
                           ).then_inc(mid4_ready, 1)
                b = batch(turn, q, 1)
                if b is not None:
                    cols, k = len(batch_windows(b)), (q - 1) % 4
                    act.wait_ge(ln_ready, turn * 4 + q)
                    act.wait_ge(slots_stored[k], batch_turn(turn, q, 1, 16))
                    a.copy(gath[:, k * BATCH:k * BATCH + cols, 0:D], resid[:, bass.ds(b * BATCH, cols), :]
                           ).then_inc(hi4_ready, 1)
                b = batch(turn, q, 3)
                if b is not None:
                    k = (q - 3) % 4
                    act.wait_ge(mid4_ready, turn * 4 + (q - 2))
                    act.wait_ge(lo4_ready, turn * 4 + (q - 2))
                    if isinstance(b, int) and b == BATCHES - 1:
                        for i, n in enumerate(batch_windows(b)):
                            act.dma_start(window_rows(table[0], n), gath[0:rows(n), k * BATCH + i, 0:PARTS * D]
                                          ).then_inc(slots_stored[i], 16)
                    else:
                        act.dma_start(window_span(table[0], b * BATCH), gath[:, k * BATCH:(k + 1) * BATCH, 0:PARTS * D]
                                      ).then_inc(slots_stored[k], 16)
            for k in range(4):
                act.sem_inc(slots_stored[k], 16)
            over_batches(act, slot_phase0, 0, BATCHES)

            act.wait_ge(w_loaded, N_WEIGHTS)

            def slot_layer0(w, half, p):
                if exists(w - 1):
                    n, r = w - 1, rows(w - 1)
                    if not isinstance(n, int) or n >= 2:
                        act.wait_ge(z_tp_ready, n - 1)
                    a.copy(xb[1 - p][0:r, :], resid[0:r, col(n), :].rearrange("p n d -> p (n d)")
                           ).then_inc(ln_copied, 1)
                if exists(w - 2):
                    n, r = w - 2, rows(w - 2)
                    act.wait_ge(z_tp_ready, n + 1)
                    if not isinstance(n, int) or n >= 2:
                        act.wait_ge(hT_ready, n - 1)
                    a.copy(zT[p][:, :, 0:r], tp[:].rearrange("p h (k n) -> p (h k) n", n=P)[:, :, 0:r]
                           ).then_inc(zT_ready, 1)
                if exists(w - 3):
                    n, r = w - 3, rows(w - 3)
                    act.wait_ge(hT_ready, n + 1)
                    if not isinstance(n, int) or n >= 2:
                        act.wait_ge(mm_ready, upto(1, n - 2))
                    for m in range(KD):
                        last = a.activation(featT[1 - p][:, m, 0:r], hT[:, m, 0:r], ACT.Relu,
                                            bias=bias0[:, m:m + 1])
                    last.then_inc(featT_ready, 1)
                if exists(w - 4):
                    split_store(1, w - 4, earlier(half, p, 4), p)
            over_windows(act, 4, slot_layer0)

            act.wait_ge(mm_ready, NT)
            act.dma_start(w1_sb, w1.rearrange("(k p) n -> p k n", p=P)).then_inc(w1_loaded, 16)

            def slot_layer1(w, half, p):
                if exists(w - 2):
                    copy_transposed(2, w - 2, p)
                if exists(w - 3):
                    split_store(2, w - 3, earlier(half, p, 3), 1 - p)
            over_windows(act, 3, slot_layer1)

            def gelu(n, p):
                r = rows(n)
                act.wait_ge(f1_ready, n + 1)
                if not isinstance(n, int) or n >= 2:
                    act.wait_ge(y_ready, n - 1)
                for j in range(KH):
                    last = a.activation(hidT[p][:, j, 0:r], hid[:, j // 4, (j % 4) * P:(j % 4) * P + r],
                                        ACT.Gelu_apprx_tanh, bias=b1_sb[:, j:j + 1])
                last.then_inc(gelu_ready, 1)

            act.wait_ge(feat_ready, turned(2, NT - 1))

            def slot_ffn(w, half, p):
                if exists(w):
                    if not isinstance(w, int) or w >= 2:
                        act.wait_ge(x1_ready, w - 1)
                    act.dma_start(xb[p][0:rows(w), :], window_rows(x, w)).then_inc(x_loaded[p], 16)
                if exists(w - 1):
                    std_dev(3, w - 1, 1 - p)
                if exists(w - 2):
                    copy_transposed(3, w - 2, p)
                if exists(w - 3):
                    gelu(w - 3, 1 - p)
                if exists(w - 4):
                    act.wait_ge(yw_ready, w - 3)
                    act.dma_start(window_rows(yw_dram, w - 4), yw[p][0:rows(w - 4), :]).then_inc(yw_stored[p], 16)
            over_windows(act, 4, slot_ffn)

            with act.Fori(0, TURNS) as it:
                for k in range(FIN_BUFS):
                    act.wait_ge(fin_ready, it * FIN_BUFS + (k + 1))
                    act.dma_start(window_span(out, it * (FIN_BUFS * BATCH) + k * BATCH), fin[k]
                                  ).then_inc(fin_stored[k], 16)
            for p, n in enumerate(range(LAST_LOOPED, NT)):
                act.wait_ge(fin_ready, FIN_BUFS * TURNS + p + 1)
                act.dma_start(window_rows(out, n), fin[p][0:rows(n), 0, :]).then_inc(fin_stored[p], 16)
            for k in range(FIN_BUFS):
                act.wait_ge(fin_stored[k], 16 * (TURNS + (k < NT - LAST_LOOPED)))


def kernel(x, src, dst, L0_gnn_W0_self, L0_gnn_W0_neigh, L0_gnn_b0, L0_gnn_W1_self, L0_gnn_W1_neigh, L0_gnn_b1,
           L0_gnn_W2_self, L0_gnn_W2_neigh, L0_gnn_b2, L0_ffn_attention_mask, L0_ffn_wr, L0_ffn_br, L0_ffn_w1,
           L0_ffn_b1, L0_ffn_w2, L0_ffn_b2):
    import concourse.bacc as bacc
    from concourse.bass_utils import run_bass_kernel_spmd

    nc = bacc.Bacc("TRN2", target_bir_lowering=False, num_devices=1)
    arrays = {}

    def give(name, a):
        a = np.ascontiguousarray(a)
        arrays[name] = a
        return nc.dram_tensor(name, a.shape, mybir.dt.from_np(a.dtype), kind="ExternalInput").ap()

    out = nc.dram_tensor("out", x.shape, F32, kind="ExternalOutput").ap()
    gnn_ffn_program(
        nc, give("x", x), give("src", src), give("dst", dst),
        [give(f"w_self{i}", w) for i, w in enumerate((L0_gnn_W0_self, L0_gnn_W1_self, L0_gnn_W2_self))],
        [give(f"w_neigh{i}", w) for i, w in enumerate((L0_gnn_W0_neigh, L0_gnn_W1_neigh, L0_gnn_W2_neigh))],
        [give(f"b_gnn{i}", b) for i, b in enumerate((L0_gnn_b0, L0_gnn_b1, L0_gnn_b2))],
        give("wr", L0_ffn_wr), give("br", L0_ffn_br), give("w1", L0_ffn_w1), give("b1", L0_ffn_b1),
        give("w2", L0_ffn_w2), give("b2", L0_ffn_b2), out)
    got = run_bass_kernel_spmd(nc, [arrays], core_ids=[0])
    return got.results[0]["out"]
```
